# Optimizing a Trainium2 kernel written in Bass

```python
import numpy as np
import jax
import jax.numpy as jnp

def _softmax(x, axis=-1):
    return jax.nn.softmax(x, axis=axis)

def _gelu(x):
    return jax.nn.gelu(x, approximate=True)

def _silu(x):
    return jax.nn.silu(x)

def _sigmoid(x):
    return jax.nn.sigmoid(x)

def _layernorm(x, axis=-1, eps=1e-05):
    m = jnp.mean(x, axis=axis, keepdims=True)
    v = jnp.var(x, axis=axis, keepdims=True)
    return (x - m) / jnp.sqrt(v + eps)

def _scatter_add(tgt, idx, src, axis=0):
    return tgt.at[idx].add(src)

def _segment_sum(src, seg, n):
    return jax.ops.segment_sum(src, seg, n)
kernel_name = 'mk_flamingo_gated_d1_seqx_r8_d09cfa'

def setup_inputs(seed: int=0):
    np.random.seed(seed)
    _w = jnp.asarray

    def _rec_inputs():
        import jax
        import jax.numpy as jnp
        _rk = jax.random.key(seed)
        x = -0.0003929 + 0.9999 * jax.random.normal(jax.random.fold_in(_rk, 1), (8, 56, 512), jnp.float32)
        _lenS = 56 - jax.random.randint(jax.random.fold_in(_rk, 7), (8,), 0, max(1, 56 // 4) + 1, jnp.int32)
        _lenS2 = 1500 - jax.random.randint(jax.random.fold_in(_rk, 8), (8,), 0, max(1, 1500 // 4) + 1, jnp.int32)
        _ctx_4096P = jax.random.normal(jax.random.fold_in(_rk, 11), (8, 16, 512), jnp.float32)
        _ctx_4096c = jax.random.dirichlet(jax.random.fold_in(_rk, 511), 0.3 * jnp.ones((16,), jnp.float32), (8, 1500))
        _ctx_4096t = jnp.einsum('bsk,bkd->bsd', _ctx_4096c, _ctx_4096P)
        _ctx_4096t = _ctx_4096t * jax.lax.rsqrt(jnp.mean(jnp.square(_ctx_4096t)) + 1e-12) * 0.953939
        ctx_4096 = 2.81802e-05 + 1.00001 * (_ctx_4096t + 0.3 * jax.random.normal(jax.random.fold_in(_rk, 611), (8, 1500, 512), jnp.float32))
        _validS = jnp.arange(56)[None, :] < _lenS[:, None]
        _validS2 = jnp.arange(1500)[None, :] < _lenS2[:, None]
        _causal = jnp.tril(jnp.ones((56, 56), dtype=bool))
        mask_BxSxS2_ff0 = jnp.where(jnp.ones((8, 56, 1500), dtype=bool), 0.0, -1000000000.0).astype(jnp.float32)
        _g = jax.random.normal(jax.random.fold_in(_rk, 9001), (2, 1), jnp.float32)
        _g = jnp.sign(_g) * jnp.maximum(jnp.abs(_g), 1.0) + (_g == 0) * 1.0
        g_xattn = _g[0]
        g_ffn = _g[1]
        return (x, ctx_4096, mask_BxSxS2_ff0, g_xattn, g_ffn)
    x, ctx_4096, mask_BxSxS2_ff0, g_xattn, g_ffn = _rec_inputs()

    def _L0_xattn_setup():
        import jax, jax.numpy as jnp
        import numpy as np
        BS, SEQ, D_MODEL = (4, 128, 512)
        N_Q_HEADS, N_KV_HEADS, D_K, D_V = (32, 8, 128, 128)
        ROPE_BASE = 10000.0

        def _rotate_half(x):
            x1, x2 = jnp.split(x, 2, axis=-1)
            return jnp.concatenate([-x2, x1], axis=-1)

        def _apply_rope(x, pos0):
            d = x.shape[-1]
            seq = x.shape[2]
            inv_freq = 1.0 / ROPE_BASE ** (jnp.arange(0, d, 2, dtype=jnp.float32) / d)
            pos = (pos0 + jnp.arange(seq)).astype(jnp.float32)
            ang = pos[:, None] * inv_freq[None, :]
            cos = jnp.concatenate([jnp.cos(ang), jnp.cos(ang)], axis=-1)
            sin = jnp.concatenate([jnp.sin(ang), jnp.sin(ang)], axis=-1)
            return x * cos[None, None] + _rotate_half(x) * sin[None, None]
        key = jax.random.key(seed)
        ks = jax.random.split(key, 8)
        w_scale = 0.02
        return {'query': jax.random.normal(ks[0], (BS, SEQ, D_MODEL), dtype=jnp.float32), 'key': jax.random.normal(ks[1], (BS, SEQ, D_MODEL), dtype=jnp.float32), 'value': jax.random.normal(ks[2], (BS, SEQ, D_MODEL), dtype=jnp.float32), 'mask': jnp.zeros((BS, SEQ, SEQ), dtype=jnp.float32), 'wq': jax.random.normal(ks[3], (D_MODEL, N_Q_HEADS * D_K), dtype=jnp.float32) * w_scale, 'wk': jax.random.normal(ks[4], (D_MODEL, N_KV_HEADS * D_K), dtype=jnp.float32) * w_scale, 'wv': jax.random.normal(ks[5], (D_MODEL, N_KV_HEADS * D_V), dtype=jnp.float32) * w_scale, 'wo': jax.random.normal(ks[6], (N_Q_HEADS * D_V, D_MODEL), dtype=jnp.float32) * w_scale, 'curr_seq_pos': 0}
    _L0_xattn_all = _L0_xattn_setup()
    _L0_xattn_in = {k: v for k, v in _L0_xattn_all.items() if k in ('wq', 'wk', 'wv', 'wo')}
    del _L0_xattn_all

    def _L0_ffn_setup():
        import jax, jax.numpy as jnp
        import numpy as np
        LORA_R = 16
        SCALE = 16.0 / np.sqrt(16.0)
        NUM_EXPERTS = 4
        TOP_K = 2
        IN_F = 512
        OUT_F = 512
        key = jax.random.key(seed)
        k_x, k_a, k_b, k_r = jax.random.split(key, 4)
        x = jax.random.normal(k_x, (2, 256, IN_F), dtype=jnp.float32)
        A = jax.random.normal(k_a, (NUM_EXPERTS, LORA_R, IN_F), dtype=jnp.float32) * (1.0 / np.sqrt(IN_F))
        B = jax.random.normal(k_b, (NUM_EXPERTS, OUT_F, LORA_R), dtype=jnp.float32) * 0.02
        Wr = jax.random.normal(k_r, (NUM_EXPERTS, IN_F), dtype=jnp.float32) * 0.02
        return {'x': x, 'A': A, 'B': B, 'Wr': Wr}
    _L0_ffn_all = _L0_ffn_setup()
    _L0_ffn_in = {k: v for k, v in _L0_ffn_all.items() if k in ('A', 'B', 'Wr')}
    del _L0_ffn_all
    return {'x': x, 'ctx_4096': ctx_4096, 'mask_BxSxS2_ff0': mask_BxSxS2_ff0, 'g_xattn': g_xattn, 'g_ffn': g_ffn, 'L0_xattn_wq': _L0_xattn_in['wq'], 'L0_xattn_wk': _L0_xattn_in['wk'], 'L0_xattn_wv': _L0_xattn_in['wv'], 'L0_xattn_wo': _L0_xattn_in['wo'], 'L0_ffn_A': _L0_ffn_in['A'], 'L0_ffn_B': _L0_ffn_in['B'], 'L0_ffn_Wr': _L0_ffn_in['Wr']}

def reference(x, ctx_4096, mask_BxSxS2_ff0, g_xattn, g_ffn, L0_xattn_wq, L0_xattn_wk, L0_xattn_wv, L0_xattn_wo, L0_ffn_A, L0_ffn_B, L0_ffn_Wr):
    import jax
    import jax.numpy as jnp

    def _L0_xattn_ref(query, key, value, mask, wq, wk, wv, wo, curr_seq_pos):
        import jax, jax.numpy as jnp
        import numpy as np
        BS, SEQ, D_MODEL = (4, 128, 512)
        N_Q_HEADS, N_KV_HEADS, D_K, D_V = (32, 8, 128, 128)
        ROPE_BASE = 10000.0

        def _rotate_half(x):
            x1, x2 = jnp.split(x, 2, axis=-1)
            return jnp.concatenate([-x2, x1], axis=-1)

        def _apply_rope(x, pos0):
            d = x.shape[-1]
            seq = x.shape[2]
            inv_freq = 1.0 / ROPE_BASE ** (jnp.arange(0, d, 2, dtype=jnp.float32) / d)
            pos = (pos0 + jnp.arange(seq)).astype(jnp.float32)
            ang = pos[:, None] * inv_freq[None, :]
            cos = jnp.concatenate([jnp.cos(ang), jnp.cos(ang)], axis=-1)
            sin = jnp.concatenate([jnp.sin(ang), jnp.sin(ang)], axis=-1)
            return x * cos[None, None] + _rotate_half(x) * sin[None, None]
        bs, sq, _ = query.shape
        n_groups = N_Q_HEADS // N_KV_HEADS
        q = (query @ wq).reshape(bs, sq, N_Q_HEADS, D_K).transpose((0, 2, 1, 3))
        sk = key.shape[1]
        k = (key @ wk).reshape(bs, sk, N_KV_HEADS, 1, D_K)
        k = jnp.repeat(k, n_groups, axis=3).reshape(bs, sk, N_Q_HEADS, D_K).transpose((0, 2, 1, 3))
        v = (value @ wv).reshape(bs, sk, N_KV_HEADS, 1, D_V)
        v = jnp.repeat(v, n_groups, axis=3).reshape(bs, sk, N_Q_HEADS, D_V).transpose((0, 2, 1, 3))
        scale = jnp.sqrt(jnp.float32(D_K))
        q = _apply_rope(q, curr_seq_pos)
        k = _apply_rope(k, curr_seq_pos)
        raw = jnp.einsum('bhqd,bhkd->bhqk', q, k) / scale
        masked = raw + mask[:bs, None, curr_seq_pos:curr_seq_pos + sq, :sk]
        attn = jax.nn.softmax(masked, axis=-1)
        out = jnp.einsum('bhqk,bhkd->bhqd', attn, v)
        out = out.transpose((0, 2, 1, 3)).reshape(bs, sq, N_Q_HEADS * D_V)
        return out @ wo

    def _L0_ffn_ref(x, A, B, Wr):
        import jax, jax.numpy as jnp
        import numpy as np
        LORA_R = 16
        SCALE = 16.0 / np.sqrt(16.0)
        NUM_EXPERTS = 4
        TOP_K = 2
        IN_F = 512
        OUT_F = 512
        orig_shape = x.shape
        flat = x.reshape(-1, orig_shape[-1])
        logits = flat @ Wr.T
        topk_vals, topk_idx = jax.lax.top_k(logits, TOP_K)
        T = flat.shape[0]
        neg_inf = jnp.finfo(logits.dtype).min
        sparse = jnp.full_like(logits, neg_inf)
        rows = jnp.arange(T)[:, None]
        sparse = sparse.at[rows, topk_idx].set(topk_vals)
        gates = jax.nn.softmax(sparse, axis=-1)
        mid = jnp.einsum('tf,erf->ter', flat, A)
        all_deltas = jnp.einsum('ter,eor->teo', mid, B) * SCALE
        delta = jnp.sum(gates[:, :, None] * all_deltas, axis=1)
        return delta.reshape(*orig_shape[:-1], -1)
    x = x + jnp.tanh(g_xattn[0]) * _L0_xattn_ref(_layernorm(x, axis=-1), ctx_4096, ctx_4096, mask_BxSxS2_ff0, L0_xattn_wq, L0_xattn_wk, L0_xattn_wv, L0_xattn_wo, 0)
    x = x + jnp.tanh(g_ffn[0]) * _L0_ffn_ref(_layernorm(x, axis=-1), L0_ffn_A, L0_ffn_B, L0_ffn_Wr)
    return x

_drawn_inputs = setup_inputs


def setup_inputs(seed=0):
    import zlib

    import numpy as np

    out = dict(_drawn_inputs(seed))
    spreads = {}
    factors = {'L0_xattn_wk': 2.892}
    for name, (base, spread) in spreads.items():
        noise = np.random.default_rng([zlib.crc32(name.encode()), seed]).standard_normal(out[name].shape)
        drawn = base * np.exp(spread * noise) if base else spread * noise
        out[name] = jnp.asarray(drawn.astype(out[name].dtype))
    for name, factor in factors.items():
        out[name] = (out[name] * factor).astype(out[name].dtype)
    return out
```

```python
from contextlib import ExitStack

import numpy as np

import concourse.bass as bass
from concourse import mybir
from concourse.alu_op_type import AluOpType as ALU

ACT = mybir.ActivationFunctionType
F32 = mybir.dt.float32
F32R = mybir.dt.float32r
AX_X = mybir.AxisListType.X

P = 128
B, SQ, D = 8, 56, 512
SK = 1500
HKV, REP, DH = 8, 4, 128
DC = D // P
HALF = DH // 2
TOK = B * SQ
ROWS = 2 * SQ
NTT = TOK // ROWS
HALVES = REP // 2
GQ = REP * SQ
GW = REP * DH
ST = 125
NT = SK // ST
SC = 500
NC = SK // SC
CT = SC // ST
PAIR = 2 * DH
VT = NT // 2
PT = NT // 2
STAGE = 3
STAGES = NT // STAGE
BANK = 512
RING = 2
PT_SLOTS = 3
EXPERTS, RANK = 4, 16
ER = EXPERTS * RANK
LORA_SCALE = 16.0 / float(np.sqrt(16.0))
EPS = 1e-5
LOWEST = -3.4e38
PASSES = ((0, 0), (1, 0), (0, 1))

K_ITEMS = HKV * NC
SV_ITEMS = HKV * HALVES * NC + (HKV // 2) * VT
T_ITEMS = HKV * PT + NT


def f32(ap):
    return ap.bitcast(F32)


def k_item(b, g, c=0):
    return b * K_ITEMS + g * NC + c


def sv_item(b, g, i=0):
    return b * SV_ITEMS + (g * HALVES * NC + ((g + 1) // 2) * VT + i)


def t_item(b, g, j, last):
    return b * T_ITEMS + (NT + g * PT + j + (NT if g == HKV - 1 and not last else 0))


def next_c_item(b):
    return b * T_ITEMS + (NT + (HKV - 1) * PT)


def wait_apart(eng, sem, value, passed):
    eng.wait_ge(sem, value)
    eng.sem_inc(passed, 1)


def query_part(nc, ctx, ident, x, wq, q_cos, q_sin, q_dram):
    def sb(name, shape, dt=F32):
        return ctx.enter_context(nc.sbuf_tensor(name, shape, dt))

    def sem(name):
        return ctx.enter_context(nc.semaphore(name))

    x_tok = sb("q_x_tok", [ROWS, NTT, D])
    stats = sb("q_stats", [ROWS, NTT, 6])
    mv = sb("q_mv", [ROWS, NTT, 2])
    var = sb("q_var", [ROWS, NTT])
    std = sb("q_std", [ROWS, NTT])
    rstd = sb("q_rstd", [ROWS, NTT])
    xn = sb("q_xn", [ROWS, NTT, D])
    xT = [sb(f"xT_{n}", [P, DC, TOK], F32R) for n in ("hi", "lo")]
    wq_raw = sb("wq_raw", [P, 2, DC, GW])
    wq_s = [sb(f"wq_{n}", [P, 2, DC, GW], F32R) for n in ("hi", "lo")]
    cos_t = sb("q_cos_t", [P, SQ])
    sin_t = sb("q_sin_t", [P, SQ])
    q_swap = sb("q_swap", [P, 2, B, SQ])
    q_part = sb("q_part", [P, 2, B, SQ])
    q_rot = sb("q_rot", [P, 2, B, REP, SQ])
    xT_banks = ctx.enter_context(nc.psum_tensor("xT_banks", [P, DC, BANK], F32))
    q_banks = ctx.enter_context(nc.psum_tensor("q_banks", [P, RING, BANK], F32))

    sp_passed = sem("q_sp_passed")
    x_loaded, tables_loaded = sem("x_loaded"), sem("q_tables_loaded")
    wq_loaded = [sem(f"wq_loaded{i}") for i in range(2)]
    q_stored = [sem(f"q_stored{i}") for i in range(2)]
    cleared, ident_ready = sem("ident_cleared"), sem("ident_ready")
    stats_ready, mv_ready, var_ready, std_ready, rstd_ready, xn_ready = (
        sem(f"q_{n}_ready") for n in ("stats", "mv", "var", "std", "rstd", "xn"))
    xT_banked, xT_hi, xT_lo = sem("xT_banked"), sem("xT_hi_ready"), sem("xT_lo_ready")
    wq_hi, wq_lo = sem("wq_hi_ready"), sem("wq_lo_ready")
    q_ready, q_free, q_swapped, q_sined, q_rotated = (
        sem(n) for n in ("q_ready", "q_free", "q_swapped", "q_sined", "q_rotated"))
    swap_free = sem("q_swap_free")

    x_v = x.rearrange("(t b) s d -> (b s) t d", t=NTT)
    wq_v = wq.rearrange("(c p) n -> p c n", p=P)
    pairs = HKV // 2
    heads2 = 2 * REP

    block = ctx.enter_context(nc.Block())

    @block.sync
    def _(sp):
        for u in range(2):
            sp.sem_inc(q_stored[u], 16)
        sp.dma_start(x_tok[:, :, :], x_v).then_inc(x_loaded, 16)
        for u in range(2):
            sp.dma_start(wq_raw[:, u], wq_v[:, :, u * GW:(u + 1) * GW]).then_inc(wq_loaded[u], 16)
        sp.dma_start(cos_t[:, :], q_cos).then_inc(tables_loaded, 16)
        sp.dma_start(sin_t[:, :], q_sin).then_inc(tables_loaded, 16)

        def two_groups(i, last):
            for u in range(2):
                if not last:
                    sp.wait_ge(wq_hi, i * 2 + (u + 1))
                    wait_apart(sp, wq_lo, i * 2 + (u + 1), sp_passed)
                    src = wq_v[:, :, bass.ds(i * (2 * GW) + (2 + u) * GW, GW)]
                    sp.dma_start(wq_raw[:, u], src).then_inc(wq_loaded[u], 16)
                wait_apart(sp, q_rotated, i * heads2 + (u + 1) * REP, sp_passed)
                dst = q_dram[bass.ds(i * 2 + u, 1)].rearrange("g p b n -> p (g b n)")
                sp.dma_start(dst, q_rot[:, u].rearrange("p b h s -> p (b h s)")).then_inc(q_stored[u], 16)

        with sp.Fori(0, pairs - 1) as i:
            two_groups(i, False)
        two_groups(pairs - 1, True)
        for u in range(2):
            sp.wait_ge(q_stored[u], 16 * (pairs + 1))

    @block.gpsimd
    def _(pool):
        nc.gpsimd.memset(ident[:, :], 0.0).then_inc(cleared, 1)
        pool.wait_ge(cleared, 1)
        nc.gpsimd.affine_select(out=ident[:, :], in_=ident[:, :], compare_op=ALU.not_equal, fill=1.0,
                                base=0, pattern=[[-1, P]], channel_multiplier=1).then_inc(ident_ready, 1)

    @block.scalar
    def _(act):
        act.wait_ge(var_ready, 1)
        nc.scalar.activation(std[:, :], var[:, :], ACT.Sqrt).then_inc(std_ready, 1)

        def split_wq(n, u):
            act.wait_ge(wq_loaded[u], (n - u) * 8 + 16)
            nc.scalar.activation(wq_s[0][:, u], wq_raw[:, u], ACT.Copy).then_inc(wq_hi, 1)

        split_wq(0, 0)
        for c in range(DC):
            act.wait_ge(xT_banked, c + 1)
            nc.scalar.activation(xT[0][:, c, :], xT_banks[:, c, 0:TOK], ACT.Copy).then_inc(xT_hi, 1)

        def two_groups(i, last):
            for u in range(2):
                for hh in range(REP):
                    act.wait_ge(q_ready, i * heads2 + (u * REP + hh + 1))
                    act.wait_ge(swap_free, i * heads2 + (u * REP + hh + 1))
                    for lo in range(2):
                        nc.scalar.activation(
                            q_swap[lo * HALF:(lo + 1) * HALF, hh % 2].rearrange("p b s -> p (b s)"),
                            q_banks[(1 - lo) * HALF:(2 - lo) * HALF, hh % 2, 0:TOK], ACT.Copy).then_inc(q_swapped, 1)
                    if hh == 1 and not (last and u == 1):
                        split_wq(i * 2 + (u + 1), 1 - u)

        with act.Fori(0, pairs - 1) as i:
            two_groups(i, False)
        two_groups(pairs - 1, True)

    @block.tensor
    def _(pe):
        pe.wait_ge(ident_ready, 1)
        for c in range(DC):
            for t in range(NTT):
                if c == 0:
                    pe.wait_ge(xn_ready, t + 1)
                mm = nc.tensor.transpose(xT_banks[:, c, t * ROWS:(t + 1) * ROWS], xn[:, t, c * P:(c + 1) * P],
                                         ident[0:ROWS, 0:ROWS])
            mm.then_inc(xT_banked, 1)
        pe.wait_ge(xT_lo, DC)

        def two_groups(i):
            for u in range(2):
                pe.wait_ge(wq_lo, i * 2 + (u + 1))
                for hh in range(REP):
                    pe.wait_ge(q_free, i * heads2 + (u * REP + hh + 1))
                    for c in range(DC):
                        for n, (a, m) in enumerate(PASSES):
                            mm = nc.tensor.matmul(q_banks[:, hh % 2, 0:TOK], wq_s[a][:, u, c, hh * DH:(hh + 1) * DH],
                                                  xT[m][:, c, :], start=(c == 0 and n == 0),
                                                  stop=(c == DC - 1 and n == len(PASSES) - 1))
                    mm.then_inc(q_ready, 1)

        with pe.Fori(0, pairs) as i:
            two_groups(i)

    @block.vector
    def _(dve):
        dve.sem_inc(q_free, RING)
        dve.sem_inc(swap_free, 2)
        dve.wait_ge(x_loaded, 16)
        for t in range(NTT):
            nc.vector.bn_stats(stats[:, t], x_tok[:, t]).then_inc(stats_ready, 1)
        for t in range(NTT):
            dve.wait_ge(stats_ready, t + 1)
            nc.vector.bn_aggr(mv[:, t], stats[:, t]).then_inc(mv_ready, 1)
        dve.wait_ge(mv_ready, NTT)
        nc.vector.tensor_scalar(var[:, :], mv[:, :, 1], EPS, None, ALU.add).then_inc(var_ready, 1)
        dve.wait_ge(std_ready, 1)
        nc.vector.reciprocal(rstd[:, :], std[:, :]).then_inc(rstd_ready, 1)
        dve.wait_ge(rstd_ready, 1)
        for t in range(NTT):
            nc.vector.tensor_scalar(xn[:, t], x_tok[:, t], mv[:, t, 0:1], rstd[:, t:t + 1],
                                    ALU.subtract, ALU.mult).then_inc(xn_ready, 1)

        def split_wq(n, u):
            dve.wait_ge(wq_hi, n + 1)
            nc.vector.tensor_tensor(wq_s[1][:, u], wq_raw[:, u], f32(wq_s[0][:, u]), ALU.subtract).then_inc(wq_lo, 1)

        split_wq(0, 0)
        for c in range(DC):
            dve.wait_ge(xT_hi, c + 1)
            nc.vector.tensor_tensor(xT[1][:, c, :], xT_banks[:, c, 0:TOK], f32(xT[0][:, c, :]),
                                    ALU.subtract).then_inc(xT_lo, 1)
        dve.wait_ge(tables_loaded, 32)
        cos_b = cos_t[:, None, :].broadcast_to([P, B, SQ])
        sin_b = sin_t[:, None, :].broadcast_to([P, B, SQ])

        def two_groups(i, last):
            for u in range(2):
                dve.wait_ge(q_stored[u], i * 16 + 16)
                for hh in range(REP):
                    n = u * REP + hh
                    s = hh % 2
                    dve.wait_ge(q_swapped, i * (2 * heads2) + 2 * (n + 1))
                    nc.vector.tensor_tensor(q_part[:, s], q_banks[:, s, 0:TOK].rearrange("p (b s) -> p b s", b=B),
                                            cos_b, ALU.mult).then_inc(q_free, 1)
                    nc.vector.tensor_tensor(q_swap[:, s], q_swap[:, s], sin_b, ALU.mult).then_inc(q_sined, 1)
                    dve.wait_ge(q_free, i * heads2 + (RING + n + 1))
                    dve.wait_ge(q_sined, i * heads2 + (n + 1))
                    nc.vector.tensor_tensor(q_rot[:, u, :, hh, :], q_part[:, s], q_swap[:, s],
                                            ALU.add).then_inc(q_rotated, 1)
                    dve.wait_ge(q_rotated, i * heads2 + (n + 1))
                    dve.sem_inc(swap_free, 1)
                    if hh == 1 and not (last and u == 1):
                        split_wq(i * 2 + (u + 1), 1 - u)

        with dve.Fori(0, pairs - 1) as i:
            two_groups(i, False)
        two_groups(pairs - 1, True)


def attention_part(nc, ctx, ident, ctx_in, mask, wk, wv, k_cos, k_sin, q_dram, attn_dram):
    def sb(name, shape, dt=F32):
        return ctx.enter_context(nc.sbuf_tensor(name, shape, dt))

    def ps(name, n):
        return ctx.enter_context(nc.psum_tensor(name, [P, n, BANK], F32))

    def sem(name):
        return ctx.enter_context(nc.semaphore(name))

    def halves(name, shape):
        return [sb(f"{name}_{h}", shape, F32R) for h in ("hi", "lo")]

    stage = sb("stage", [P, 2, STAGE * D])
    cT = halves("cT", [P, DC, SK])
    w = [halves("wk", [P, DC, HKV * DH]), halves("wv", [P, DC, HKV * DH])]
    v = halves("v", [ST, NT, PAIR])
    k = halves("k", [P, SK])
    k_swap = sb("k_swap", [P, 2, SC])
    k_rot = sb("k_rot", [P, 2, SC])
    cos_t, sin_t = sb("k_cos_t", [P, SK]), sb("k_sin_t", [P, SK])
    mask_t = sb("mask_t", [ROWS, SK])
    prob = [sb(f"prob{h}", [ROWS, SK]) for h in range(HALVES)]
    pT = halves("pT", [ST, PT_SLOTS, 2 * GQ])
    q_raw = sb("q_raw", [P, 2, GQ])
    q = halves("q", [P, GQ])
    chunk_max = sb("chunk_max", [ROWS, HALVES, NC])
    neg_max = sb("neg_max", [ROWS, HALVES])
    row_sum = sb("row_sum", [ROWS, HALVES])
    inv_sum = sb("inv_sum", [ROWS, HALVES])
    inv_b = sb("inv_b", [P, GQ])
    attn = sb("attn", [P, 2, GQ])
    k_banks, sv_banks, t_banks, o_banks = ps("k_banks", RING), ps("sv_banks", RING), ps("t_banks", RING), ps("o_banks", RING)

    stage_loaded = [sem(f"stage_loaded{i}") for i in range(2)]
    q_loaded = [sem(f"q_loaded{i}") for i in range(2)]
    attn_stored = [sem(f"attn_stored{i}") for i in range(2)]
    tables_loaded, mask_loaded = sem("k_tables_loaded"), sem("mask_loaded")
    sp_passed, dve_passed = sem("sp_passed"), sem("dve_passed")
    w_hi, w_lo = sem("w_hi_ready"), sem("w_lo_ready")
    sv_ready, sv_free, v_hi = sem("sv_ready"), sem("sv_free"), sem("v_hi_ready")
    k_ready, k_swapped, k_free, k_sined, k_rotated, k_hi, k_lo = (
        sem(n) for n in ("k_ready", "k_swapped", "k_free", "k_sined", "k_rotated", "k_hi_ready", "k_lo_ready"))
    t_ready, t_hi, t_free = sem("t_ready"), sem("t_hi_ready"), sem("t_free")
    o_ready, o_free, inv_copied = sem("o_ready"), sem("o_free"), sem("inv_copied")
    max_ready, p_ready, inv_ready = sem("max_ready"), sem("p_ready"), sem("inv_ready")
    q_hi, q_lo = sem("q_hi_ready"), sem("q_lo_ready")

    W_PIECES = 2 * DC
    w_loads = W_PIECES // 2
    c_loads = STAGES // 2
    ctx_v = ctx_in.rearrange("b (k t p) d -> b k p t d", k=STAGES, p=ST)
    steps2 = HKV // 2

    def c_stage_ready(eng, b, m):
        n = m // STAGE
        eng.wait_ge(stage_loaded[n % 2], b * (16 * c_loads) + 16 * (w_loads + n // 2 + 1))

    def c_tile(m):
        return stage[0:ST, (m // STAGE) % 2, (m % STAGE) * D:(m % STAGE + 1) * D]

    block = ctx.enter_context(nc.Block())

    @block.sync
    def _(sp):
        def load_context(b, n):
            sp.dma_start(stage[0:ST, n % 2].rearrange("p (t d) -> p t d", t=STAGE),
                         ctx_v[bass.ds(b, 1), n].rearrange("b p t d -> p (b t) d")).then_inc(stage_loaded[n % 2], 16)

        def load_mask(b):
            for r in range(2):
                sp.dma_start(mask_t[r * SQ:(r + 1) * SQ, :],
                             mask[bass.ds(b, 1)].rearrange("b s n -> (b s) n")).then_inc(mask_loaded, 16)

        def load_q(b, g):
            sp.dma_start(q_raw[:, g % 2], q_dram[g, :, bass.ds(b, 1)].rearrange("p b n -> p (b n)")).then_inc(q_loaded[g % 2], 16)

        for s in range(2):
            sp.sem_inc(attn_stored[s], 16)
        for n in range(W_PIECES):
            if n >= 2:
                sp.wait_ge(w_lo, n - 1)
            src = (wk, wv)[n // DC]
            c = n % DC
            sp.dma_start(stage[:, n % 2, 0:HKV * DH], src[c * P:(c + 1) * P, :]).then_inc(stage_loaded[n % 2], 16)
            if n == 1:
                sp.dma_start(cos_t[:, :], k_cos).then_inc(tables_loaded, 16)
                sp.dma_start(sin_t[:, :], k_sin).then_inc(tables_loaded, 16)
        load_q(0, 0)
        load_q(0, 1)
        load_mask(0)
        for n in range(STAGES):
            if n < 2:
                sp.wait_ge(w_lo, W_PIECES - 1 + n)
            else:
                sp.wait_ge(t_ready, (n - 1) * STAGE)
            load_context(0, n)

        def batch(b, last):
            if not last:
                for n in range(2):
                    wait_apart(sp, t_ready, b * T_ITEMS + NT, sp_passed)
                    load_context(b + 1, n)
            for g in range(HKV):
                if g + 2 < HKV or not last:
                    wait_apart(sp, q_lo, b * HKV + (g + 1), sp_passed)
                    load_q(b + (g + 2) // HKV, (g + 2) % HKV)
                if g == HKV - 1 and not last:
                    wait_apart(sp, sv_free, RING + sv_item(b, g, HALVES * NC), sp_passed)
                    load_mask(b + 1)
                    for n in range(2, STAGES):
                        wait_apart(sp, t_ready, next_c_item(b) + (n - 1) * STAGE, sp_passed)
                        load_context(b + 1, n)
                wait_apart(sp, o_free, b * HKV + (RING + g + 1), sp_passed)
                sp.dma_start(attn_dram[g, :, bass.ds(b, 1)].rearrange("p b n -> p (b n)"), attn[:, g % 2]).then_inc(attn_stored[g % 2], 16)

        with sp.Fori(0, B - 1) as b:
            batch(b, False)
        batch(B - 1, True)
        for s in range(2):
            sp.wait_ge(attn_stored[s], 16 * (B * steps2 + 1))

    @block.gpsimd
    def _(pool):
        def k_low(item, s, c):
            pool.wait_ge(k_hi, item + 1)
            nc.gpsimd.tensor_tensor(k[1][:, c * SC:(c + 1) * SC], k_rot[:, s], f32(k[0][:, c * SC:(c + 1) * SC]),
                                    ALU.subtract).then_inc(k_lo, 1)

        for c in range(NC):
            k_low(k_item(0, 0, c), c % 2, c)

        def batch(b, last):
            for g in range(1, HKV + 1 - last):
                for c in range(NC):
                    k_low(k_item(b, g, c), (g * NC + c) % 2, c)

        with pool.Fori(0, B - 1) as b:
            batch(b, False)
        batch(B - 1, True)

    @block.scalar
    def _(act):
        def k_exchange(item, s):
            act.wait_ge(k_ready, item + 1)
            if not isinstance(item, int) or item >= 2:
                act.wait_ge(k_rotated, item - 1)
            for lo in range(2):
                nc.scalar.activation(k_swap[lo * HALF:(lo + 1) * HALF, s],
                                     k_banks[(1 - lo) * HALF:(2 - lo) * HALF, s, 0:SC], ACT.Copy).then_inc(k_swapped, 1)

        def k_high(item, s, c):
            act.wait_ge(k_rotated, item + 1)
            nc.scalar.activation(k[0][:, c * SC:(c + 1) * SC], k_rot[:, s], ACT.Copy).then_inc(k_hi, 1)

        def c_high(item, m):
            act.wait_ge(t_ready, item + m + 1)
            nc.scalar.activation(cT[0][:, :, m * ST:(m + 1) * ST],
                                 t_banks[:, m % 2, 0:DC * ST].rearrange("p (c s) -> p c s", c=DC), ACT.Copy).then_inc(t_hi, 1)

        def context(first_t, first_k):
            for m in range(2 * CT + 1):
                c_high(first_t, m)
            k_exchange(first_k, 0)
            for m in range(2 * CT + 1, NT):
                c_high(first_t, m)
            k_exchange(first_k + 1, 1)

        def q_high(b, g):
            n = g % 2
            act.wait_ge(q_loaded[n], b * (16 * steps2) + 16 * (g // 2 + 1))
            nc.scalar.activation(q[0][:, :], q_raw[:, n], ACT.Copy).then_inc(q_hi, 1)

        for n in range(W_PIECES):
            act.wait_ge(stage_loaded[n % 2], 16 * (n // 2 + 1))
            nc.scalar.activation(w[n // DC][0][:, n % DC, :], stage[:, n % 2, 0:HKV * DH], ACT.Copy).then_inc(w_hi, 1)
        q_high(0, 0)
        context(0, 0)
        k_high(0, 0, 0)
        k_high(1, 1, 1)
        k_exchange(2, 0)
        k_high(2, 0, 2)

        def batch(b, last):
            for g in range(HKV):
                more = g + 1 < HKV or not last
                kn = k_item(b, g + 1)
                s0 = (g + 1) * NC % 2

                def p_high(j):
                    act.wait_ge(t_ready, t_item(b, g, j, last) + 1)
                    nc.scalar.activation(pT[0][:, j % PT_SLOTS, :], t_banks[0:ST, j % 2, 0:2 * GQ], ACT.Copy).then_inc(t_hi, 1)

                for h in range(HALVES):
                    act.wait_ge(max_ready, b * (HKV * HALVES) + (g * HALVES + h + 1))
                    nc.scalar.activation(prob[h][:, :], prob[h][:, :], ACT.Exp, bias=neg_max[:, h:h + 1],
                                         accum_out=row_sum[:, h:h + 1]).then_inc(p_ready, 1)
                if more:
                    q_high(b, g + 1)
                if g % 2 == 0:
                    for m in range(VT):
                        act.wait_ge(sv_ready, sv_item(b, g, HALVES * NC + m) + 1)
                        nc.scalar.activation(v[0][:, 2 * m:2 * m + 2, :],
                                             sv_banks[0:ST, m % 2, :].rearrange("p (t n) -> p t n", t=2), ACT.Copy).then_inc(v_hi, 1)
                if g == HKV - 1 and more:
                    context(next_c_item(b), kn)
                elif more:
                    k_exchange(kn, s0)
                    k_exchange(kn + 1, 1 - s0)
                p_high(0)
                if more:
                    k_high(kn, s0, 0)
                p_high(1)
                if more:
                    k_high(kn + 1, 1 - s0, 1)
                    k_exchange(kn + 2, s0)
                p_high(2)
                p_high(3)
                if more:
                    k_high(kn + 2, s0, 2)
                p_high(4)
                p_high(5)

        with act.Fori(0, B - 1) as b:
            batch(b, False)
        batch(B - 1, True)

    @block.tensor
    def _(pe):
        def k_part(item, s, g, c, d):
            for n, (a, m) in enumerate(PASSES):
                mm = nc.tensor.matmul(k_banks[:, s, 0:SC], w[0][a][:, d, g * DH:(g + 1) * DH],
                                      cT[m][:, d, c * SC:(c + 1) * SC], start=(d == 0 and n == 0),
                                      stop=(d == DC - 1 and n == len(PASSES) - 1))
            if d == DC - 1:
                mm.then_inc(k_ready, 1)

        def k_chunk(item, s, g, c):
            pe.wait_ge(k_free, item + 1)
            for d in range(DC):
                k_part(item, s, g, c, d)

        def context(b, first_t, first_k):
            for m in range(NT):
                pe.wait_ge(t_free, first_t + m + 1)
                if m % STAGE == 0:
                    c_stage_ready(pe, b, m)
                for d in range(DC):
                    mm = nc.tensor.transpose(t_banks[:, m % 2, d * ST:(d + 1) * ST], c_tile(m)[:, d * P:(d + 1) * P],
                                             ident[0:ST, 0:ST])
                mm.then_inc(t_ready, 1)
                if m >= CT:
                    c, d = divmod(m - CT, DC)
                    if d == 0:
                        pe.wait_ge(k_free, first_k + c + 1)
                        pe.wait_ge(t_free, first_t + (RING + (c + 1) * CT))
                    k_part(first_k + c, c, 0, c, d)

        def k_last(first_t, first_k, c=NC - 1):
            pe.wait_ge(t_free, first_t + (RING + NT))
            k_chunk(first_k + c, 0, 0, c)

        pe.wait_ge(w_lo, W_PIECES)
        context(0, 0, 0)
        k_last(0, 0)

        def batch(b, last):
            for g in range(HKV):
                more = g + 1 < HKV or not last
                kn = k_item(b, g + 1)
                s0 = (g + 1) * NC % 2

                def transposes(j):
                    n = t_item(b, g, j, last)
                    pe.wait_ge(t_free, n + 1)
                    if j == 0:
                        pe.wait_ge(p_ready, b * (HKV * HALVES) + (g + 1) * HALVES)
                    for t in range(2):
                        for h in range(HALVES):
                            col = t * GQ + h * ROWS
                            mm = nc.tensor.transpose(t_banks[0:ST, j % 2, col:col + ROWS],
                                                     prob[h][:, (2 * j + t) * ST:(2 * j + t + 1) * ST],
                                                     ident[0:ROWS, 0:ROWS])
                    mm.then_inc(t_ready, 1)

                def weigh(j):
                    pe.wait_ge(t_free, t_item(b, g, j, last) + (RING + 1))
                    if j == 0 and g % 2 == 0:
                        pe.wait_ge(sv_free, sv_item(b, g, HALVES * NC + VT) + RING)
                    for t in range(2):
                        for n, (a, m) in enumerate(PASSES):
                            mm = nc.tensor.matmul(o_banks[:, g % 2, 0:GQ],
                                                  v[a][:, 2 * j + t, (g % 2) * DH:(g % 2 + 1) * DH],
                                                  pT[m][:, j % PT_SLOTS, t * GQ:(t + 1) * GQ],
                                                  start=(j == 0 and t == 0 and n == 0),
                                                  stop=(j == PT - 1 and t == 1 and n == len(PASSES) - 1))
                    if j == PT - 1:
                        mm.then_inc(o_ready, 1)

                pe.wait_ge(q_lo, b * HKV + (g + 1))
                for h in range(HALVES):
                    for c in range(NC):
                        i = h * NC + c
                        pe.wait_ge(sv_free, sv_item(b, g, i) + 1)
                        if h == 0:
                            pe.wait_ge(k_lo, k_item(b, g, c) + 1)
                        for n, (a, m) in enumerate(PASSES):
                            mm = nc.tensor.matmul(sv_banks[0:ROWS, i % 2, 0:SC], q[a][:, h * ROWS:(h + 1) * ROWS],
                                                  k[m][:, c * SC:(c + 1) * SC], start=(n == 0), stop=(n == len(PASSES) - 1))
                        mm.then_inc(sv_ready, 1)
                if g % 2 == 0:
                    for m in range(VT):
                        pe.wait_ge(sv_free, sv_item(b, g, HALVES * NC + m) + 1)
                        for t in range(2):
                            tile = 2 * m + t
                            for d in range(DC):
                                for n, (a, mv) in enumerate(PASSES):
                                    mm = nc.tensor.matmul(sv_banks[0:ST, m % 2, t * PAIR:(t + 1) * PAIR],
                                                          cT[a][:, d, tile * ST:(tile + 1) * ST],
                                                          w[1][mv][:, d, g * DH:g * DH + PAIR],
                                                          start=(d == 0 and n == 0),
                                                          stop=(d == DC - 1 and n == len(PASSES) - 1))
                        mm.then_inc(sv_ready, 1)
                if g == HKV - 1 and more:
                    context(b + 1, next_c_item(b), kn)
                elif more:
                    k_chunk(kn, s0, g + 1, 0)
                    k_chunk(kn + 1, 1 - s0, g + 1, 1)
                transposes(0)
                transposes(1)
                pe.wait_ge(o_free, b * HKV + (g + 1))
                pe.wait_ge(inv_ready, b * (HKV * HALVES) + (g + 1) * HALVES)
                for h in range(HALVES):
                    nc.tensor.transpose(o_banks[:, g % 2, GQ + h * ROWS:GQ + (h + 1) * ROWS],
                                        inv_sum[:, h:h + 1].broadcast_to([ROWS, P]), ident[0:ROWS, 0:ROWS])
                if g == HKV - 1 and more:
                    k_last(next_c_item(b), kn)
                elif more:
                    k_chunk(kn + 2, s0, g + 1, 2)
                transposes(2)
                weigh(0)
                transposes(3)
                weigh(1)
                transposes(4)
                weigh(2)
                transposes(5)
                weigh(3)
                weigh(4)
                weigh(5)

        with pe.Fori(0, B - 1) as b:
            batch(b, False)
        batch(B - 1, True)

    @block.vector
    def _(dve):
        for ring in (k_free, sv_free, t_free, o_free):
            dve.sem_inc(ring, RING)

        def k_cos_part(item, s, c):
            dve.wait_ge(k_swapped, item * 2 + 2)
            if not isinstance(item, int) or item >= 2:
                dve.wait_ge(k_lo, item - 1)
            nc.vector.tensor_tensor(k_rot[:, s], k_banks[:, s, 0:SC], cos_t[:, c * SC:(c + 1) * SC],
                                    ALU.mult).then_inc(k_free, 1)

        def k_rotate(item, s, c):
            nc.vector.tensor_tensor(k_swap[:, s], k_swap[:, s], sin_t[:, c * SC:(c + 1) * SC],
                                    ALU.mult).then_inc(k_sined, 1)
            dve.wait_ge(k_free, item + (RING + 1))
            dve.wait_ge(k_sined, item + 1)
            nc.vector.tensor_tensor(k_rot[:, s], k_rot[:, s], k_swap[:, s], ALU.add).then_inc(k_rotated, 1)

        def c_low(item, m):
            dve.wait_ge(t_hi, item + m + 1)
            dst = slice(m * ST, (m + 1) * ST)
            nc.vector.tensor_tensor(cT[1][:, :, dst], t_banks[:, m % 2, 0:DC * ST].rearrange("p (c s) -> p c s", c=DC),
                                    f32(cT[0][:, :, dst]), ALU.subtract).then_inc(t_free, 1)

        def context(first_t, first_k):
            for m in range(2 * CT + 1):
                c_low(first_t, m)
            k_cos_part(first_k, 0, 0)
            k_rotate(first_k, 0, 0)
            for m in range(2 * CT + 1, NT):
                c_low(first_t, m)

        def q_low(b, g):
            dve.wait_ge(q_hi, b * HKV + (g + 1))
            nc.vector.tensor_tensor(q[1][:, :], q_raw[:, g % 2], f32(q[0][:, :]), ALU.subtract).then_inc(q_lo, 1)

        for n in range(W_PIECES):
            dve.wait_ge(w_hi, n + 1)
            nc.vector.tensor_tensor(w[n // DC][1][:, n % DC, :], stage[:, n % 2, 0:HKV * DH],
                                    f32(w[n // DC][0][:, n % DC, :]), ALU.subtract).then_inc(w_lo, 1)
        q_low(0, 0)
        dve.wait_ge(tables_loaded, 32)
        context(0, 0)
        for c in (1, 2):
            k_cos_part(c, c % 2, c)
            k_rotate(c, c % 2, c)

        def batch(b, last):
            dve.wait_ge(mask_loaded, b * 32 + 32)
            for g in range(HKV):
                more = g + 1 < HKV or not last
                kn = k_item(b, g + 1)
                s0 = (g + 1) * NC % 2

                def p_low(j):
                    dve.wait_ge(t_hi, t_item(b, g, j, last) + 1)
                    nc.vector.tensor_tensor(pT[1][:, j % PT_SLOTS, :], t_banks[0:ST, j % 2, 0:2 * GQ],
                                            f32(pT[0][:, j % PT_SLOTS, :]), ALU.subtract).then_inc(t_free, 1)

                for h in range(HALVES):
                    for c in range(NC):
                        i = h * NC + c
                        wait_apart(dve, sv_ready, sv_item(b, g, i) + 1, dve_passed)
                        nc.vector.tensor_tensor_reduce(prob[h][:, c * SC:(c + 1) * SC], sv_banks[0:ROWS, i % 2, 0:SC],
                                                       mask_t[:, c * SC:(c + 1) * SC], 1.0, LOWEST, ALU.add, ALU.max,
                                                       chunk_max[:, h, c:c + 1]).then_inc(sv_free, 1)
                    dve.wait_ge(sv_free, sv_item(b, g, (h + 1) * NC) + RING)
                    nc.vector.tensor_reduce(neg_max[:, h:h + 1], chunk_max[:, h, :], AX_X, ALU.max,
                                            negate=True).then_inc(max_ready, 1)
                if more:
                    q_low(b, g + 1)
                if g % 2 == 0:
                    for m in range(VT):
                        dve.wait_ge(v_hi, b * (steps2 * VT) + (g // 2 * VT + m + 1))
                        nc.vector.tensor_tensor(v[1][:, 2 * m:2 * m + 2, :],
                                                sv_banks[0:ST, m % 2, :].rearrange("p (t n) -> p t n", t=2),
                                                f32(v[0][:, 2 * m:2 * m + 2, :]), ALU.subtract).then_inc(sv_free, 1)
                if g == HKV - 1 and more:
                    context(next_c_item(b), kn)
                elif more:
                    k_cos_part(kn, s0, 0)
                    k_rotate(kn, s0, 0)
                for h in range(HALVES):
                    dve.wait_ge(p_ready, b * (HKV * HALVES) + (g * HALVES + h + 1))
                    nc.vector.reciprocal(inv_sum[:, h:h + 1], row_sum[:, h:h + 1]).then_inc(inv_ready, 1)
                p_low(0)
                p_low(1)
                if more:
                    k_cos_part(kn + 1, 1 - s0, 1)
                    k_rotate(kn + 1, 1 - s0, 1)
                p_low(2)
                if more:
                    k_cos_part(kn + 2, s0, 2)
                p_low(3)
                if more:
                    k_rotate(kn + 2, s0, 2)
                p_low(4)
                p_low(5)
                dve.wait_ge(o_ready, b * HKV + (g + 1))
                dve.wait_ge(o_free, b * HKV + (RING + g))
                nc.vector.tensor_copy(inv_b[:, :], o_banks[:, g % 2, GQ:2 * GQ]).then_inc(inv_copied, 1)
                dve.wait_ge(inv_copied, b * HKV + (g + 1))
                dve.wait_ge(attn_stored[g % 2], b * (16 * steps2) + 16 * (g // 2 + 1))
                nc.vector.tensor_tensor(attn[:, g % 2], o_banks[:, g % 2, 0:GQ], inv_b[:, :], ALU.mult).then_inc(o_free, 1)

        with dve.Fori(0, B - 1) as b:
            batch(b, False)
        batch(B - 1, True)


def output_part(nc, ctx, ident, x, wo, a_in, b_in, wr, g_xattn, g_ffn, attn_dram, out):
    def sb(name, shape, dt=F32):
        return ctx.enter_context(nc.sbuf_tensor(name, shape, dt))

    def sem(name):
        return ctx.enter_context(nc.semaphore(name))

    attn_raw = sb("attn_raw", [P, 2, B, REP, SQ])
    attn_s = [sb(f"attn_{n}", [P, 2, REP, B, SQ], F32R) for n in ("hi", "lo")]
    wo_raw = sb("wo_raw", [P, 2, REP, D])
    wo_s = [sb(f"wo_{n}", [P, 2, REP, D], F32R) for n in ("hi", "lo")]
    x_tok = sb("o_x_tok", [ROWS, NTT, D])
    y = sb("y", [ROWS, NTT, D])
    yn = sb("yn", [ROWS, NTT, D])
    res = sb("res", [ROWS, NTT, D])
    gate_raw = sb("gate_raw", [ROWS, 2])
    tanh_g = sb("tanh_g", [ROWS, 2])
    ar = sb("ar", [ER + EXPERTS, D])
    arT = sb("arT", [P, DC, ER + EXPERTS])
    b_raw = sb("b_raw", [P, DC, EXPERTS, RANK])
    bT = sb("bT", [ER, D])
    stats = sb("o_stats", [ROWS, NTT, 6])
    mv = sb("o_mv", [ROWS, NTT, 2])
    var = sb("o_var", [ROWS, NTT])
    std = sb("o_std", [ROWS, NTT])
    rstd = sb("o_rstd", [ROWS, NTT])
    yT = sb("yT", [P, DC, TOK])
    z = sb("z", [ROWS, NTT, ER + EXPERTS])
    earlier = sb("earlier", [ROWS, NTT, EXPERTS, EXPERTS])
    beats = sb("beats", [ROWS, NTT, EXPERTS, EXPERTS])
    ties = sb("ties", [ROWS, NTT, EXPERTS, EXPERTS])
    rank = sb("rank", [ROWS, NTT, EXPERTS])
    top = sb("top", [ROWS, NTT])
    shifted = sb("shifted", [ROWS, NTT, EXPERTS])
    gates = sb("gates", [ROWS, NTT, EXPERTS])
    total = sb("total", [ROWS, NTT])
    inv_total = sb("inv_total", [ROWS, NTT])
    mid = sb("mid", [ROWS, NTT, EXPERTS, RANK])
    midT = sb("midT", [ER, TOK])
    acc = ctx.enter_context(nc.psum_tensor("acc", [P, NTT, BANK], F32))
    yT_banks = ctx.enter_context(nc.psum_tensor("yT_banks", [P, DC, BANK], F32))

    attn_loaded = [sem(f"attn_loaded{i}") for i in range(2)]
    wo_loaded = [sem(f"wo_loaded{i}") for i in range(2)]
    sp_passed = sem("o_sp_passed")
    x_loaded, small_loaded = sem("o_x_loaded"), sem("small_loaded")
    attn_hi, attn_lo, wo_hi, wo_lo = sem("attn_hi_ready"), sem("attn_lo_ready"), sem("wo_hi_ready"), sem("wo_lo_ready")
    group_done, tanh_ready, y_ready = sem("group_done"), sem("tanh_ready"), sem("y_ready")
    stats_ready, mv_ready, var_ready, std_ready, rstd_ready, yn_ready = (
        sem(f"o_{n}_ready") for n in ("stats", "mv", "var", "std", "rstd", "yn"))
    small_banked, small_copied = sem("small_banked"), sem("small_copied")
    yT_banked, yT_ready, z_banked, z_ready = sem("yT_banked"), sem("yT_ready"), sem("z_banked"), sem("z_ready")
    gate_steps, earlier_steps, exp_ready, mid_ready = sem("gate_steps"), sem("earlier_steps"), sem("exp_ready"), sem("mid_ready")
    midT_banked, midT_ready, delta_ready, res_ready, stored = (
        sem(n) for n in ("midT_banked", "midT_ready", "delta_ready", "res_ready", "stored"))

    x_v = x.rearrange("(t b) s d -> (b s) t d", t=NTT)
    out_v = out.rearrange("(t b) s d -> (b s) t d", t=NTT)
    wo_v = wo.rearrange("(g h p) n -> g p h n", h=REP, p=P)
    pairs = HKV // 2
    SMALL = 16 * (4 + DC)

    block = ctx.enter_context(nc.Block())

    @block.sync
    def _(sp):
        def load_group(g, u):
            sp.dma_start(attn_raw[:, u].rearrange("p b h s -> p (b h s)"),
                         attn_dram[bass.ds(g, 1)].rearrange("g p b n -> p (g b n)")).then_inc(attn_loaded[u], 16)
            sp.dma_start(wo_raw[:, u], wo_v[bass.ds(g, 1)].rearrange("g p h n -> p (g h) n")).then_inc(wo_loaded[u], 16)

        load_group(0, 0)
        load_group(1, 1)
        sp.dma_start(x_tok[:, :, :], x_v).then_inc(x_loaded, 16)
        with nc.allow_non_contiguous_dma("small operands"):
            sp.dma_start(ar[0:ER, :], a_in.rearrange("e r f -> (e r) f")).then_inc(small_loaded, 16)
            sp.dma_start(ar[ER:ER + EXPERTS, :], wr).then_inc(small_loaded, 16)
            for n, gate in enumerate((g_xattn, g_ffn)):
                sp.dma_start(gate_raw[:, n:n + 1], gate.rearrange("(a n) -> a n", a=1).broadcast_to([ROWS, 1])).then_inc(small_loaded, 16)
            for c in range(DC):
                sp.dma_start(b_raw[:, c], b_in[:, c * P:(c + 1) * P, :].rearrange("e o r -> o e r")).then_inc(small_loaded, 16)

        def two_groups(i):
            for u in range(2):
                sp.wait_ge(attn_lo, i * 2 + (u + 1))
                wait_apart(sp, wo_lo, i * 2 + (u + 1), sp_passed)
                load_group(i * 2 + (2 + u), u)

        with sp.Fori(0, pairs - 1) as i:
            two_groups(i)
        for t in range(NTT):
            sp.wait_ge(res_ready, t + 1)
            sp.dma_start(out_v[:, t], res[:, t]).then_inc(stored, 16)
        sp.wait_ge(stored, 16 * NTT)

    @block.gpsimd
    def _(pool):
        nc.gpsimd.memset(earlier[:, :, :, :], 1.0).then_inc(earlier_steps, 1)
        pool.wait_ge(earlier_steps, 1)
        nc.gpsimd.affine_select(out=earlier[:, :, :, :], in_=earlier[:, :, :, :], compare_op=ALU.is_gt, fill=0.0, base=0,
                                pattern=[[0, NTT], [1, EXPERTS], [-1, EXPERTS]], channel_multiplier=0).then_inc(earlier_steps, 1)

    @block.scalar
    def _(act):
        def split_group(n, u, needs_use):
            act.wait_ge(attn_loaded[u], (n - u) * 8 + 16)
            if needs_use:
                act.wait_ge(group_done, n - 1)
            nc.scalar.activation(attn_s[0][:, u].rearrange("p h b s -> p b h s"), attn_raw[:, u], ACT.Copy).then_inc(attn_hi, 1)
            act.wait_ge(wo_loaded[u], (n - u) * 8 + 16)
            nc.scalar.activation(wo_s[0][:, u], wo_raw[:, u], ACT.Copy).then_inc(wo_hi, 1)

        for u in range(2):
            split_group(u, u, False)
        with act.Fori(1, pairs) as i:
            for u in range(2):
                split_group(i * 2 + u, u, True)
        act.wait_ge(small_loaded, SMALL)
        nc.scalar.activation(tanh_g[:, :], gate_raw[:, :], ACT.Tanh).then_inc(tanh_ready, 1)
        act.wait_ge(var_ready, 1)
        nc.scalar.activation(std[:, :], var[:, :], ACT.Sqrt).then_inc(std_ready, 1)
        for c in range(0, DC, 2):
            act.wait_ge(yT_banked, c + 1)
            nc.scalar.activation(yT[:, c, :], yT_banks[:, c, 0:TOK], ACT.Copy).then_inc(yT_ready, 1)
        act.wait_ge(gate_steps, 4)
        nc.scalar.activation(gates[:, :, :], shifted[:, :, :], ACT.Exp).then_inc(exp_ready, 1)

    @block.tensor
    def _(pe):
        def group(g, u, first, last):
            pe.wait_ge(attn_lo, g + 1)
            pe.wait_ge(wo_lo, g + 1)
            for h in range(REP):
                for t in range(NTT):
                    for n, (a, m) in enumerate(PASSES):
                        mm = nc.tensor.matmul(acc[0:ROWS, t, :],
                                              attn_s[a][:, u, h].rearrange("p b s -> p (b s)")[:, t * ROWS:(t + 1) * ROWS],
                                              wo_s[m][:, u, h, :], start=(first and h == 0 and n == 0),
                                              stop=(last and h == REP - 1 and n == len(PASSES) - 1), skip_group_check=True)
            mm.then_inc(group_done, 1)

        group(0, 0, True, False)
        group(1, 1, False, False)
        with pe.Fori(1, pairs - 1) as i:
            for u in range(2):
                group(i * 2 + u, u, False, False)
        group(HKV - 2, 0, False, False)
        group(HKV - 1, 1, False, True)

        pe.wait_ge(small_loaded, SMALL)
        n = ER + EXPERTS
        for c in range(DC):
            mm = nc.tensor.transpose(yT_banks[:, 0, c * n:(c + 1) * n], ar[:, c * P:(c + 1) * P], ident[0:n, 0:n])
        mm.then_inc(small_banked, 1)
        for c in range(DC):
            mm = nc.tensor.transpose(yT_banks[0:ER, 1, c * P:(c + 1) * P], b_raw[:, c].rearrange("p e r -> p (e r)"), ident[:, :])
        mm.then_inc(small_banked, 1)
        pe.wait_ge(small_copied, 2)
        for c in range(DC):
            for t in range(NTT):
                if c == 0:
                    pe.wait_ge(yn_ready, t + 1)
                mm = nc.tensor.transpose(yT_banks[:, c, t * ROWS:(t + 1) * ROWS], yn[:, t, c * P:(c + 1) * P], ident[0:ROWS, 0:ROWS])
            mm.then_inc(yT_banked, 1)
        pe.wait_ge(yT_ready, DC)
        for t in range(NTT):
            for c in range(DC):
                mm = nc.tensor.matmul(acc[0:ROWS, 0, t * n:(t + 1) * n], yT[:, c, t * ROWS:(t + 1) * ROWS], arT[:, c, :],
                                      start=(c == 0), stop=(c == DC - 1))
        mm.then_inc(z_banked, 1)
        pe.wait_ge(mid_ready, 1)
        for t in range(NTT):
            mm = nc.tensor.transpose(yT_banks[0:ER, 0, t * ROWS:(t + 1) * ROWS], mid[:, t].rearrange("p e r -> p (e r)"), ident[0:ROWS, 0:ROWS])
        mm.then_inc(midT_banked, 1)
        pe.wait_ge(midT_ready, 1)
        for t in range(NTT):
            nc.tensor.matmul(acc[0:ROWS, t, :], midT[:, t * ROWS:(t + 1) * ROWS], bT[:, :], start=True, stop=True).then_inc(delta_ready, 1)

    @block.vector
    def _(dve):
        def split_group(n, u):
            dve.wait_ge(attn_hi, n + 1)
            nc.vector.tensor_tensor(attn_s[1][:, u].rearrange("p h b s -> p b h s"), attn_raw[:, u],
                                    f32(attn_s[0][:, u]).rearrange("p h b s -> p b h s"), ALU.subtract).then_inc(attn_lo, 1)
            dve.wait_ge(wo_hi, n + 1)
            nc.vector.tensor_tensor(wo_s[1][:, u], wo_raw[:, u], f32(wo_s[0][:, u]), ALU.subtract).then_inc(wo_lo, 1)

        with dve.Fori(0, pairs) as i:
            for u in range(2):
                split_group(i * 2 + u, u)
        dve.wait_ge(small_banked, 1)
        nc.vector.tensor_copy(arT[:, :, :], yT_banks[:, 0, 0:DC * (ER + EXPERTS)].rearrange("p (c n) -> p c n", c=DC)).then_inc(small_copied, 1)
        dve.wait_ge(small_banked, 2)
        nc.vector.tensor_copy(bT[:, :], yT_banks[0:ER, 1, :]).then_inc(small_copied, 1)
        dve.wait_ge(x_loaded, 16)
        dve.wait_ge(tanh_ready, 1)
        dve.wait_ge(group_done, HKV)
        for t in range(NTT):
            nc.vector.scalar_tensor_tensor(out=y[:, t], in0=acc[0:ROWS, t, :], scalar=tanh_g[:, 0:1], in1=x_tok[:, t],
                                           op0=ALU.mult, op1=ALU.add).then_inc(y_ready, 1)
        for t in range(NTT):
            dve.wait_ge(y_ready, t + 1)
            nc.vector.bn_stats(stats[:, t], y[:, t]).then_inc(stats_ready, 1)
        for t in range(NTT):
            dve.wait_ge(stats_ready, t + 1)
            nc.vector.bn_aggr(mv[:, t], stats[:, t]).then_inc(mv_ready, 1)
        dve.wait_ge(mv_ready, NTT)
        nc.vector.tensor_scalar(var[:, :], mv[:, :, 1], EPS, None, ALU.add).then_inc(var_ready, 1)
        dve.wait_ge(std_ready, 1)
        nc.vector.reciprocal(rstd[:, :], std[:, :]).then_inc(rstd_ready, 1)
        dve.wait_ge(rstd_ready, 1)
        for t in range(NTT):
            nc.vector.tensor_scalar(yn[:, t], y[:, t], mv[:, t, 0:1], rstd[:, t:t + 1], ALU.subtract, ALU.mult).then_inc(yn_ready, 1)
        for c in range(1, DC, 2):
            dve.wait_ge(yT_banked, c + 1)
            nc.vector.tensor_copy(yT[:, c, :], yT_banks[:, c, 0:TOK]).then_inc(yT_ready, 1)
        dve.wait_ge(z_banked, 1)
        nc.vector.tensor_copy(z[:, :, :], acc[0:ROWS, 0, 0:NTT * (ER + EXPERTS)].rearrange("p (t n) -> p t n", t=NTT)).then_inc(z_ready, 1)
        dve.wait_ge(z_ready, 1)
        logits = z[:, :, ER:ER + EXPERTS]
        square = [ROWS, NTT, EXPERTS, EXPERTS]
        of_e = logits[:, :, :, None].broadcast_to(square)
        of_j = logits[:, :, None, :].broadcast_to(square)
        nc.vector.tensor_reduce(top[:, :], logits, AX_X, ALU.max).then_inc(gate_steps, 1)
        nc.vector.tensor_tensor(beats[:, :, :, :], of_j, of_e, ALU.is_gt).then_inc(gate_steps, 1)
        nc.vector.tensor_tensor(ties[:, :, :, :], of_j, of_e, ALU.is_equal).then_inc(gate_steps, 1)
        dve.wait_ge(gate_steps, 3)
        nc.vector.tensor_tensor(shifted[:, :, :], logits, top[:, :, None].broadcast_to([ROWS, NTT, EXPERTS]), ALU.subtract).then_inc(gate_steps, 1)
        dve.wait_ge(earlier_steps, 2)
        nc.vector.tensor_tensor(ties[:, :, :, :], ties[:, :, :, :], earlier[:, :, :, :], ALU.mult).then_inc(gate_steps, 1)
        dve.wait_ge(gate_steps, 5)
        nc.vector.tensor_tensor(beats[:, :, :, :], beats[:, :, :, :], ties[:, :, :, :], ALU.add).then_inc(gate_steps, 1)
        dve.wait_ge(gate_steps, 6)
        nc.vector.tensor_reduce(rank[:, :, :], beats[:, :, :, :], AX_X, ALU.add).then_inc(gate_steps, 1)
        dve.wait_ge(gate_steps, 7)
        nc.vector.tensor_scalar(rank[:, :, :], rank[:, :, :], 2.0, None, ALU.is_lt).then_inc(gate_steps, 1)
        dve.wait_ge(gate_steps, 8)
        dve.wait_ge(exp_ready, 1)
        nc.vector.tensor_tensor(gates[:, :, :], gates[:, :, :], rank[:, :, :], ALU.mult).then_inc(gate_steps, 1)
        dve.wait_ge(gate_steps, 9)
        nc.vector.tensor_reduce(total[:, :], gates[:, :, :], AX_X, ALU.add).then_inc(gate_steps, 1)
        dve.wait_ge(gate_steps, 10)
        nc.vector.reciprocal(inv_total[:, :], total[:, :]).then_inc(gate_steps, 1)
        dve.wait_ge(gate_steps, 11)
        nc.vector.tensor_tensor(gates[:, :, :], gates[:, :, :], inv_total[:, :, None].broadcast_to([ROWS, NTT, EXPERTS]), ALU.mult).then_inc(gate_steps, 1)
        dve.wait_ge(gate_steps, 12)
        nc.vector.tensor_scalar(gates[:, :, :], gates[:, :, :], LORA_SCALE, None, ALU.mult).then_inc(gate_steps, 1)
        dve.wait_ge(gate_steps, 13)
        for t in range(NTT):
            mm = nc.vector.tensor_tensor(mid[:, t], z[:, t, 0:ER].rearrange("p (e r) -> p e r", e=EXPERTS),
                                         gates[:, t, :, None].broadcast_to([ROWS, EXPERTS, RANK]), ALU.mult)
        mm.then_inc(mid_ready, 1)
        dve.wait_ge(midT_banked, 1)
        nc.vector.tensor_copy(midT[:, :], yT_banks[0:ER, 0, 0:TOK]).then_inc(midT_ready, 1)
        for t in range(NTT):
            dve.wait_ge(delta_ready, t + 1)
            nc.vector.scalar_tensor_tensor(out=res[:, t], in0=acc[0:ROWS, t, :], scalar=tanh_g[:, 1:2], in1=y[:, t],
                                           op0=ALU.mult, op1=ALU.add).then_inc(res_ready, 1)


def flamingo_block(nc, x, ctx_in, mask, g_xattn, g_ffn, wq, wk, wv, wo, a_in, b_in, wr,
                   q_cos, q_sin, k_cos, k_sin, out):
    q_dram = nc.dram_tensor("q_by_head", (HKV, P, B, GQ), F32).ap()
    attn_dram = nc.dram_tensor("attn_by_head", (HKV, P, B, GQ), F32).ap()
    with ExitStack() as whole:
        ident = whole.enter_context(nc.sbuf_tensor("ident", [P, P], F32))
        with ExitStack() as ctx:
            query_part(nc, ctx, ident, x, wq, q_cos, q_sin, q_dram)
        with ExitStack() as ctx:
            attention_part(nc, ctx, ident, ctx_in, mask, wk, wv, k_cos, k_sin, q_dram, attn_dram)
        with ExitStack() as ctx:
            output_part(nc, ctx, ident, x, wo, a_in, b_in, wr, g_xattn, g_ffn, attn_dram, out)


def rotary_tables(positions, scale):
    inv_freq = (1.0 / np.float32(10000.0) ** (np.arange(0, DH, 2, dtype=np.float32) / np.float32(DH))).astype(np.float32)
    ang = (inv_freq[:, None] * np.arange(positions, dtype=np.float32)[None, :]).astype(np.float32)
    cos, sin = np.cos(ang).astype(np.float32), np.sin(ang).astype(np.float32)
    return (np.concatenate([cos, cos]) * np.float32(scale)).astype(np.float32), \
        (np.concatenate([-sin, sin]) * np.float32(scale)).astype(np.float32)


_INS = ['x', 'ctx_4096', 'mask_BxSxS2_ff0', 'g_xattn', 'g_ffn', 'L0_xattn_wq', 'L0_xattn_wk', 'L0_xattn_wv',
        'L0_xattn_wo', 'L0_ffn_A', 'L0_ffn_B', 'L0_ffn_Wr']
_OUTS = [((B, SQ, D), 'float32')]


def kernel(**inputs):
    import numpy as _np
    import concourse.bacc as _bacc
    from concourse import mybir as _mybir
    from concourse.bass_utils import run_bass_kernel_spmd as _run

    nc = _bacc.Bacc("TRN2", target_bir_lowering=False, num_devices=1, dynamic_dma_scratch_size=1024)
    given = {name: _np.ascontiguousarray(inputs[name]) for name in _INS}
    given["q_cos"], given["q_sin"] = rotary_tables(SQ, 1.0 / _np.sqrt(_np.float32(DH)))
    given["k_cos"], given["k_sin"] = rotary_tables(SK, 1.0)
    arrays, args = {}, []
    for name, a in given.items():
        arrays[f"in_{name}_dram"] = a
        args.append(nc.dram_tensor(f"in_{name}_dram", a.shape, _mybir.dt.from_np(a.dtype), kind="ExternalInput").ap())
    for i, (shape, dtype) in enumerate(_OUTS):
        dt = _mybir.dt.from_np(_np.dtype(dtype))
        args.append(nc.dram_tensor(f"out_{i}_dram", shape, dt, kind="ExternalOutput").ap())
    flamingo_block(nc, *args)
    r = _run(nc, [arrays], core_ids=[0])
    got = tuple(r.results[0][f"out_{i}_dram"] for i in range(len(_OUTS)))
    return got[0]
```

```python
from contextlib import ExitStack

import numpy as np

import concourse.bass as bass
from concourse import mybir
from concourse.alu_op_type import AluOpType as ALU

ACT = mybir.ActivationFunctionType
F32 = mybir.dt.float32
F32R = mybir.dt.float32r
AX_X = mybir.AxisListType.X

P = 128
B, SQ, D = 8, 56, 512
SK = 1500
HKV, REP, DH = 8, 4, 128
DC = D // P
HALF = DH // 2
TOK = B * SQ
ROWS = 2 * SQ
NTT = TOK // ROWS
HALVES = REP // 2
GQ = REP * SQ
GW = REP * DH
ST = 125
NT = SK // ST
SC = 500
NC = SK // SC
CT = SC // ST
PAIR = 2 * DH
VT = NT // 2
PT = NT // 2
STAGE = 3
STAGES = NT // STAGE
BANK = 512
RING = 2
PT_SLOTS = 3
EXPERTS, RANK = 4, 16
ER = EXPERTS * RANK
LORA_SCALE = 16.0 / float(np.sqrt(16.0))
EPS = 1e-5
LOWEST = -3.4e38
PASSES = ((0, 0), (1, 0), (0, 1))

V_AHEAD = 4
V_REST = VT - V_AHEAD
SCORES = HALVES * NC

K_ITEMS = HKV * NC
SV_ITEMS = HKV * SCORES + (HKV // 2) * VT
T_ITEMS = HKV * PT + NT

K_1 = "K10 K11 K12 K13 "
V_FILLED = "V00 T3 PV1 V01 T4 PV2 V10 T5 PV3 V11 V20 PV4 V21 V30 V31 PV5"
PE_STEP = {
    "even": ("S0 S1 K00 S2 K01 S3 K02 S4 S5 K03 " + K_1 + "V40 V41 T0 K20 T1 K21 T2 inv PV0 K22 K23 "
             "T3 PV1 V50 T4 V51 PV2 T5 PV3 PV4 PV5"),
    "odd": "S0 S1 K00 S2 K01 S3 K02 S4 S5 K03 " + K_1 + "K20 K21 T0 K22 T1 K23 T2 inv PV0 " + V_FILLED,
    "turn": ("S0 S1 C0 S2 C1 S3 C2 S4 C3 S5 C4 C5 K00 C6 K01 C7 K02 C8 K03 C9 K10 C10 K11 C11 K12 K13 "
             "T0 K20 T1 K21 T2 K22 inv PV0 K23 " + V_FILLED),
    "last": "S0 S1 S2 S3 S4 S5 T0 T1 inv T2 PV0 T3 PV1 T4 PV2 T5 PV3 PV4 PV5",
    "first": "C0 C1 C2 C3 C4 K00 C5 K01 C6 K02 C7 K03 C8 K10 C9 K11 C10 K12 C11 K13 K20 K21 K22 K23 "
             "V00 V01 V10 V11 V20 V21 V30 V31",
}
ACT_STEP = {
    "even": "exp0 swap0 exp1 Q swap1 K0 V4 T0 K1 T1 T2 swap2 T3 K2 T4 V5 T5",
    "odd": "exp0 swap0 exp1 Q swap1 K0 T0 K1 T1 swap2 T2 K2 T3 V0 T4 T5 V1 V2 V3",
    "turn": ("C0 C1 exp0 C2 C3 exp1 Q C4 C5 C6 C7 C8 swap0 C9 C10 K0 C11 swap1 T0 K1 T1 swap2 T2 K2 T3 "
             "V0 T4 T5 V1 V2 V3"),
    "last": "exp0 exp1 T0 T1 T2 T3 T4 T5",
    "first": "Q C0 C1 C2 C3 C4 C5 C6 C7 C8 swap0 C9 C10 K0 C11 swap1 K1 swap2 V0 K2 V1 V2 V3",
}
DVE_STEP = {
    "even": ("mask0 mask1 mask2 max0 mask3 mask4 mask5 max1 cos0 rot0 inv Q cos1 rot1 V4 T0 T1 T2 cos2 T3 "
             "rot2 T4 V5 T5 out"),
    "odd": ("mask0 mask1 mask2 max0 mask3 mask4 mask5 max1 cos0 rot0 inv Q cos1 rot1 T0 T1 cos2 rot2 T2 T3 "
            "V0 T4 T5 V1 V2 V3 out"),
    "turn": ("mask0 mask1 C0 mask2 max0 mask3 C1 mask4 C2 mask5 max1 C3 Q inv C4 C5 C6 C7 C8 cos0 rot0 C9 C10 "
             "C11 cos1 rot1 T0 T1 cos2 rot2 T2 T3 V0 T4 T5 V1 V2 V3 out"),
    "last": "mask0 mask1 mask2 max0 mask3 mask4 mask5 max1 inv T0 T1 T2 T3 T4 T5 out",
    "first": "Q C0 C1 C2 C3 C4 C5 C6 C7 C8 cos0 rot0 C9 C10 C11 cos1 rot1 V0 cos2 rot2 V1 V2 V3",
}


def step_kind(g, last):
    return ("last" if last else "turn") if g == HKV - 1 else ("odd" if g % 2 else "even")


def tasks(order):
    for word in order.split():
        what = word.rstrip("0123456789")
        digits = word[len(what):]
        numbers = tuple(int(x) for x in digits) if what in ("K", "V") else (int(digits),) if digits else (0,)
        yield what, numbers


def f32(ap):
    return ap.bitcast(F32)


def k_item(b, g, c=0):
    return b * K_ITEMS + g * NC + c


def sv_item(b, g, i=0):
    return b * SV_ITEMS + (V_AHEAD + (g // 2) * (2 * SCORES + VT) + (g % 2) * (SCORES + V_REST) + i)


def v_fill(g, m):
    return m - (0 if g % 2 else V_AHEAD)


def t_item(b, g, j, last):
    return b * T_ITEMS + (NT + g * PT + j + (NT if g == HKV - 1 and not last else 0))


def next_c_item(b):
    return b * T_ITEMS + (NT + (HKV - 1) * PT)


def wait_apart(eng, sem, value, passed):
    eng.wait_ge(sem, value)
    eng.sem_inc(passed, 1)


def query_part(nc, ctx, ident, x, wq, q_cos, q_sin, q_dram):
    def sb(name, shape, dt=F32):
        return ctx.enter_context(nc.sbuf_tensor(name, shape, dt))

    def sem(name):
        return ctx.enter_context(nc.semaphore(name))

    x_tok = sb("q_x_tok", [ROWS, NTT, D])
    stats = sb("q_stats", [ROWS, NTT, 6])
    mv = sb("q_mv", [ROWS, NTT, 2])
    var = sb("q_var", [ROWS, NTT])
    std = sb("q_std", [ROWS, NTT])
    rstd = sb("q_rstd", [ROWS, NTT])
    xn = sb("q_xn", [ROWS, NTT, D])
    xT = [sb(f"xT_{n}", [P, DC, TOK], F32R) for n in ("hi", "lo")]
    wq_raw = sb("wq_raw", [P, 2, DC, GW])
    wq_s = [sb(f"wq_{n}", [P, 2, DC, GW], F32R) for n in ("hi", "lo")]
    cos_t = sb("q_cos_t", [P, SQ])
    sin_t = sb("q_sin_t", [P, SQ])
    q_swap = sb("q_swap", [P, 2, B, SQ])
    q_part = sb("q_part", [P, 2, B, SQ])
    q_rot = sb("q_rot", [P, 2, B, REP, SQ])
    xT_banks = ctx.enter_context(nc.psum_tensor("xT_banks", [P, DC, BANK], F32))
    q_banks = ctx.enter_context(nc.psum_tensor("q_banks", [P, RING, BANK], F32))

    sp_passed = sem("q_sp_passed")
    x_loaded, tables_loaded = sem("x_loaded"), sem("q_tables_loaded")
    wq_loaded = [sem(f"wq_loaded{i}") for i in range(2)]
    q_stored = [sem(f"q_stored{i}") for i in range(2)]
    cleared, ident_ready = sem("ident_cleared"), sem("ident_ready")
    stats_ready, mv_ready, var_ready, std_ready, rstd_ready, xn_ready = (
        sem(f"q_{n}_ready") for n in ("stats", "mv", "var", "std", "rstd", "xn"))
    xT_banked, xT_hi, xT_lo = sem("xT_banked"), sem("xT_hi_ready"), sem("xT_lo_ready")
    wq_hi, wq_lo = sem("wq_hi_ready"), sem("wq_lo_ready")
    q_ready, q_free, q_swapped, q_sined, q_rotated = (
        sem(n) for n in ("q_ready", "q_free", "q_swapped", "q_sined", "q_rotated"))
    swap_free = sem("q_swap_free")

    x_v = x.rearrange("(t b) s d -> (b s) t d", t=NTT)
    wq_v = wq.rearrange("(c p) n -> p c n", p=P)
    pairs = HKV // 2
    heads2 = 2 * REP

    block = ctx.enter_context(nc.Block())

    @block.sync
    def _(sp):
        for u in range(2):
            sp.sem_inc(q_stored[u], 16)
        sp.dma_start(x_tok[:, :, :], x_v).then_inc(x_loaded, 16)
        for u in range(2):
            sp.dma_start(wq_raw[:, u], wq_v[:, :, u * GW:(u + 1) * GW]).then_inc(wq_loaded[u], 16)
        sp.dma_start(cos_t[:, :], q_cos).then_inc(tables_loaded, 16)
        sp.dma_start(sin_t[:, :], q_sin).then_inc(tables_loaded, 16)

        def two_groups(i, last):
            for u in range(2):
                if not last:
                    sp.wait_ge(wq_hi, i * 2 + (u + 1))
                    wait_apart(sp, wq_lo, i * 2 + (u + 1), sp_passed)
                    src = wq_v[:, :, bass.ds(i * (2 * GW) + (2 + u) * GW, GW)]
                    sp.dma_start(wq_raw[:, u], src).then_inc(wq_loaded[u], 16)
                wait_apart(sp, q_rotated, i * heads2 + (u + 1) * REP, sp_passed)
                dst = q_dram[bass.ds(i * 2 + u, 1)].rearrange("g p b n -> p (g b n)")
                sp.dma_start(dst, q_rot[:, u].rearrange("p b h s -> p (b h s)")).then_inc(q_stored[u], 16)

        with sp.Fori(0, pairs - 1) as i:
            two_groups(i, False)
        two_groups(pairs - 1, True)
        for u in range(2):
            sp.wait_ge(q_stored[u], 16 * (pairs + 1))

    @block.gpsimd
    def _(pool):
        nc.gpsimd.memset(ident[:, :], 0.0).then_inc(cleared, 1)
        pool.wait_ge(cleared, 1)
        nc.gpsimd.affine_select(out=ident[:, :], in_=ident[:, :], compare_op=ALU.not_equal, fill=1.0,
                                base=0, pattern=[[-1, P]], channel_multiplier=1).then_inc(ident_ready, 1)

    @block.scalar
    def _(act):
        act.wait_ge(var_ready, 1)
        nc.scalar.activation(std[:, :], var[:, :], ACT.Sqrt).then_inc(std_ready, 1)

        def split_wq(n, u):
            act.wait_ge(wq_loaded[u], (n - u) * 8 + 16)
            nc.scalar.activation(wq_s[0][:, u], wq_raw[:, u], ACT.Copy).then_inc(wq_hi, 1)

        split_wq(0, 0)
        for c in range(DC):
            act.wait_ge(xT_banked, c + 1)
            nc.scalar.activation(xT[0][:, c, :], xT_banks[:, c, 0:TOK], ACT.Copy).then_inc(xT_hi, 1)

        def two_groups(i, last):
            for u in range(2):
                for hh in range(REP):
                    act.wait_ge(q_ready, i * heads2 + (u * REP + hh + 1))
                    act.wait_ge(swap_free, i * heads2 + (u * REP + hh + 1))
                    for lo in range(2):
                        nc.scalar.activation(
                            q_swap[lo * HALF:(lo + 1) * HALF, hh % 2].rearrange("p b s -> p (b s)"),
                            q_banks[(1 - lo) * HALF:(2 - lo) * HALF, hh % 2, 0:TOK], ACT.Copy).then_inc(q_swapped, 1)
                    if hh == 1 and not (last and u == 1):
                        split_wq(i * 2 + (u + 1), 1 - u)

        with act.Fori(0, pairs - 1) as i:
            two_groups(i, False)
        two_groups(pairs - 1, True)

    @block.tensor
    def _(pe):
        pe.wait_ge(ident_ready, 1)
        for c in range(DC):
            for t in range(NTT):
                if c == 0:
                    pe.wait_ge(xn_ready, t + 1)
                mm = nc.tensor.transpose(xT_banks[:, c, t * ROWS:(t + 1) * ROWS], xn[:, t, c * P:(c + 1) * P],
                                         ident[0:ROWS, 0:ROWS])
            mm.then_inc(xT_banked, 1)
        pe.wait_ge(xT_lo, DC)

        def two_groups(i):
            for u in range(2):
                pe.wait_ge(wq_lo, i * 2 + (u + 1))
                for hh in range(REP):
                    pe.wait_ge(q_free, i * heads2 + (u * REP + hh + 1))
                    for c in range(DC):
                        for n, (a, m) in enumerate(PASSES):
                            mm = nc.tensor.matmul(q_banks[:, hh % 2, 0:TOK], wq_s[a][:, u, c, hh * DH:(hh + 1) * DH],
                                                  xT[m][:, c, :], start=(c == 0 and n == 0),
                                                  stop=(c == DC - 1 and n == len(PASSES) - 1))
                    mm.then_inc(q_ready, 1)

        with pe.Fori(0, pairs) as i:
            two_groups(i)

    @block.vector
    def _(dve):
        dve.sem_inc(q_free, RING)
        dve.sem_inc(swap_free, 2)
        dve.wait_ge(x_loaded, 16)
        for t in range(NTT):
            nc.vector.bn_stats(stats[:, t], x_tok[:, t]).then_inc(stats_ready, 1)
        for t in range(NTT):
            dve.wait_ge(stats_ready, t + 1)
            nc.vector.bn_aggr(mv[:, t], stats[:, t]).then_inc(mv_ready, 1)
        dve.wait_ge(mv_ready, NTT)
        nc.vector.tensor_scalar(var[:, :], mv[:, :, 1], EPS, None, ALU.add).then_inc(var_ready, 1)
        dve.wait_ge(std_ready, 1)
        nc.vector.reciprocal(rstd[:, :], std[:, :]).then_inc(rstd_ready, 1)
        dve.wait_ge(rstd_ready, 1)
        for t in range(NTT):
            nc.vector.tensor_scalar(xn[:, t], x_tok[:, t], mv[:, t, 0:1], rstd[:, t:t + 1],
                                    ALU.subtract, ALU.mult).then_inc(xn_ready, 1)

        def split_wq(n, u):
            dve.wait_ge(wq_hi, n + 1)
            nc.vector.tensor_tensor(wq_s[1][:, u], wq_raw[:, u], f32(wq_s[0][:, u]), ALU.subtract).then_inc(wq_lo, 1)

        split_wq(0, 0)
        for c in range(DC):
            dve.wait_ge(xT_hi, c + 1)
            nc.vector.tensor_tensor(xT[1][:, c, :], xT_banks[:, c, 0:TOK], f32(xT[0][:, c, :]),
                                    ALU.subtract).then_inc(xT_lo, 1)
        dve.wait_ge(tables_loaded, 32)
        cos_b = cos_t[:, None, :].broadcast_to([P, B, SQ])
        sin_b = sin_t[:, None, :].broadcast_to([P, B, SQ])

        def two_groups(i, last):
            for u in range(2):
                dve.wait_ge(q_stored[u], i * 16 + 16)
                for hh in range(REP):
                    n = u * REP + hh
                    s = hh % 2
                    dve.wait_ge(q_swapped, i * (2 * heads2) + 2 * (n + 1))
                    nc.vector.tensor_tensor(q_part[:, s], q_banks[:, s, 0:TOK].rearrange("p (b s) -> p b s", b=B),
                                            cos_b, ALU.mult).then_inc(q_free, 1)
                    nc.vector.tensor_tensor(q_swap[:, s], q_swap[:, s], sin_b, ALU.mult).then_inc(q_sined, 1)
                    dve.wait_ge(q_free, i * heads2 + (RING + n + 1))
                    dve.wait_ge(q_sined, i * heads2 + (n + 1))
                    nc.vector.tensor_tensor(q_rot[:, u, :, hh, :], q_part[:, s], q_swap[:, s],
                                            ALU.add).then_inc(q_rotated, 1)
                    dve.wait_ge(q_rotated, i * heads2 + (n + 1))
                    dve.sem_inc(swap_free, 1)
                    if hh == 1 and not (last and u == 1):
                        split_wq(i * 2 + (u + 1), 1 - u)

        with dve.Fori(0, pairs - 1) as i:
            two_groups(i, False)
        two_groups(pairs - 1, True)


def attention_part(nc, ctx, ident, ctx_in, mask, wk, wv, k_cos, k_sin, q_dram, attn_dram):
    def sb(name, shape, dt=F32):
        return ctx.enter_context(nc.sbuf_tensor(name, shape, dt))

    def ps(name, n):
        return ctx.enter_context(nc.psum_tensor(name, [P, n, BANK], F32))

    def sem(name):
        return ctx.enter_context(nc.semaphore(name))

    def halves(name, shape):
        return [sb(f"{name}_{h}", shape, F32R) for h in ("hi", "lo")]

    stage = sb("stage", [P, 2, STAGE * D])
    cT = halves("cT", [P, DC, SK])
    w = [halves("wk", [P, DC, HKV * DH]), halves("wv", [P, DC, HKV * DH])]
    v = halves("v", [ST, NT, PAIR])
    k = halves("k", [P, SK])
    k_swap = sb("k_swap", [P, 2, SC])
    k_rot = sb("k_rot", [P, 2, SC])
    cos_t, sin_t = sb("k_cos_t", [P, SK]), sb("k_sin_t", [P, SK])
    mask_t = sb("mask_t", [ROWS, SK])
    prob = [sb(f"prob{h}", [ROWS, SK]) for h in range(HALVES)]
    pT = halves("pT", [ST, PT_SLOTS, 2 * GQ])
    q_raw = sb("q_raw", [P, 2, GQ])
    q = halves("q", [P, GQ])
    chunk_max = sb("chunk_max", [ROWS, HALVES, NC])
    neg_max = sb("neg_max", [ROWS, HALVES])
    row_sum = sb("row_sum", [ROWS, HALVES])
    inv_sum = sb("inv_sum", [ROWS, HALVES])
    inv_b = sb("inv_b", [P, GQ])
    attn = sb("attn", [P, 2, GQ])
    k_banks, sv_banks, t_banks, o_banks = ps("k_banks", RING), ps("sv_banks", RING), ps("t_banks", RING), ps("o_banks", RING)

    stage_loaded = [sem(f"stage_loaded{i}") for i in range(2)]
    q_loaded = [sem(f"q_loaded{i}") for i in range(2)]
    attn_stored = [sem(f"attn_stored{i}") for i in range(2)]
    tables_loaded, mask_loaded = sem("k_tables_loaded"), sem("mask_loaded")
    sp_passed, dve_passed = sem("sp_passed"), sem("dve_passed")
    w_hi, w_lo = sem("w_hi_ready"), sem("w_lo_ready")
    sv_ready, sv_free, v_hi = sem("sv_ready"), sem("sv_free"), sem("v_hi_ready")
    k_ready, k_swapped, k_free, k_sined, k_rotated, k_hi, k_lo = (
        sem(n) for n in ("k_ready", "k_swapped", "k_free", "k_sined", "k_rotated", "k_hi_ready", "k_lo_ready"))
    t_ready, t_hi, t_free = sem("t_ready"), sem("t_hi_ready"), sem("t_free")
    o_ready, o_free, inv_copied = sem("o_ready"), sem("o_free"), sem("inv_copied")
    max_ready, p_ready, inv_ready = sem("max_ready"), sem("p_ready"), sem("inv_ready")
    q_hi, q_lo = sem("q_hi_ready"), sem("q_lo_ready")

    W_PIECES = 2 * DC
    w_loads = W_PIECES // 2
    c_loads = STAGES // 2
    ctx_v = ctx_in.rearrange("b (k t p) d -> b k p t d", k=STAGES, p=ST)
    steps2 = HKV // 2

    def c_stage_ready(eng, b, m):
        n = m // STAGE
        eng.wait_ge(stage_loaded[n % 2], b * (16 * c_loads) + 16 * (w_loads + n // 2 + 1))

    def c_tile(m):
        return stage[0:ST, (m // STAGE) % 2, (m % STAGE) * D:(m % STAGE + 1) * D]

    block = ctx.enter_context(nc.Block())

    @block.sync
    def _(sp):
        def load_context(b, n):
            sp.dma_start(stage[0:ST, n % 2].rearrange("p (t d) -> p t d", t=STAGE),
                         ctx_v[bass.ds(b, 1), n].rearrange("b p t d -> p (b t) d")).then_inc(stage_loaded[n % 2], 16)

        def load_mask(b):
            for r in range(2):
                sp.dma_start(mask_t[r * SQ:(r + 1) * SQ, :],
                             mask[bass.ds(b, 1)].rearrange("b s n -> (b s) n")).then_inc(mask_loaded, 16)

        def load_q(b, g):
            sp.dma_start(q_raw[:, g % 2], q_dram[g, :, bass.ds(b, 1)].rearrange("p b n -> p (b n)")).then_inc(q_loaded[g % 2], 16)

        for s in range(2):
            sp.sem_inc(attn_stored[s], 16)
        for n in range(W_PIECES):
            if n >= 2:
                sp.wait_ge(w_lo, n - 1)
            src = (wk, wv)[n // DC]
            c = n % DC
            sp.dma_start(stage[:, n % 2, 0:HKV * DH], src[c * P:(c + 1) * P, :]).then_inc(stage_loaded[n % 2], 16)
            if n == 1:
                sp.dma_start(cos_t[:, :], k_cos).then_inc(tables_loaded, 16)
                sp.dma_start(sin_t[:, :], k_sin).then_inc(tables_loaded, 16)
        load_q(0, 0)
        load_q(0, 1)
        load_mask(0)
        for n in range(STAGES):
            if n < 2:
                sp.wait_ge(w_lo, W_PIECES - 1 + n)
            else:
                sp.wait_ge(t_ready, (n - 1) * STAGE)
            load_context(0, n)

        def batch(b, last):
            if not last:
                for n in range(2):
                    wait_apart(sp, t_ready, b * T_ITEMS + NT, sp_passed)
                    load_context(b + 1, n)
            for g in range(HKV):
                if g + 2 < HKV or not last:
                    wait_apart(sp, q_lo, b * HKV + (g + 1), sp_passed)
                    load_q(b + (g + 2) // HKV, (g + 2) % HKV)
                if g == HKV - 1 and not last:
                    for n in range(2, STAGES):
                        wait_apart(sp, t_ready, next_c_item(b) + (n - 1) * STAGE, sp_passed)
                        load_context(b + 1, n)
                    wait_apart(sp, sv_free, RING + sv_item(b, g, SCORES), sp_passed)
                    load_mask(b + 1)
                wait_apart(sp, o_free, b * HKV + (RING + g + 1), sp_passed)
                sp.dma_start(attn_dram[g, :, bass.ds(b, 1)].rearrange("p b n -> p (b n)"), attn[:, g % 2]).then_inc(attn_stored[g % 2], 16)

        with sp.Fori(0, B - 1) as b:
            batch(b, False)
        batch(B - 1, True)
        for s in range(2):
            sp.wait_ge(attn_stored[s], 16 * (B * steps2 + 1))

    @block.gpsimd
    def _(pool):
        def k_low(item, s, c):
            pool.wait_ge(k_hi, item + 1)
            nc.gpsimd.tensor_tensor(k[1][:, c * SC:(c + 1) * SC], k_rot[:, s], f32(k[0][:, c * SC:(c + 1) * SC]),
                                    ALU.subtract).then_inc(k_lo, 1)

        for c in range(NC):
            k_low(k_item(0, 0, c), c % 2, c)

        def batch(b, last):
            for g in range(1, HKV + 1 - last):
                for c in range(NC):
                    k_low(k_item(b, g, c), (g * NC + c) % 2, c)

        with pool.Fori(0, B - 1) as b:
            batch(b, False)
        batch(B - 1, True)

    @block.scalar
    def _(act):
        def k_exchange(item, s):
            act.wait_ge(k_ready, item + 1)
            if not isinstance(item, int) or item >= 2:
                act.wait_ge(k_rotated, item - 1)
            for lo in range(2):
                nc.scalar.activation(k_swap[lo * HALF:(lo + 1) * HALF, s],
                                     k_banks[(1 - lo) * HALF:(2 - lo) * HALF, s, 0:SC], ACT.Copy).then_inc(k_swapped, 1)

        def k_high(item, s, c):
            act.wait_ge(k_rotated, item + 1)
            nc.scalar.activation(k[0][:, c * SC:(c + 1) * SC], k_rot[:, s], ACT.Copy).then_inc(k_hi, 1)

        def c_high(item, m):
            act.wait_ge(t_ready, item + m + 1)
            nc.scalar.activation(cT[0][:, :, m * ST:(m + 1) * ST],
                                 t_banks[:, m % 2, 0:DC * ST].rearrange("p (c s) -> p c s", c=DC), ACT.Copy).then_inc(t_hi, 1)

        def q_high(b, g):
            n = g % 2
            act.wait_ge(q_loaded[n], b * (16 * steps2) + 16 * (g // 2 + 1))
            nc.scalar.activation(q[0][:, :], q_raw[:, n], ACT.Copy).then_inc(q_hi, 1)

        def v_high(item, m):
            act.wait_ge(sv_ready, item + 1)
            nc.scalar.activation(v[0][:, 2 * m:2 * m + 2, :],
                                 sv_banks[0:ST, m % 2, :].rearrange("p (t n) -> p t n", t=2), ACT.Copy).then_inc(v_hi, 1)

        for n in range(W_PIECES):
            act.wait_ge(stage_loaded[n % 2], 16 * (n // 2 + 1))
            nc.scalar.activation(w[n // DC][0][:, n % DC, :], stage[:, n % 2, 0:HKV * DH], ACT.Copy).then_inc(w_hi, 1)
        for what, (n, *_) in tasks(ACT_STEP["first"]):
            if what == "Q":
                q_high(0, 0)
            if what == "C":
                c_high(0, n)
            if what == "swap":
                k_exchange(n, n % 2)
            if what == "K":
                k_high(n, n % 2, n)
            if what == "V":
                v_high(n, n)

        def step(b, g, last):
            kn = k_item(b, g + 1)
            for what, (n, *_) in tasks(ACT_STEP[step_kind(g, last)]):
                s = ((g + 1) * NC + n) % 2
                if what == "exp":
                    act.wait_ge(max_ready, b * (HKV * HALVES) + (g * HALVES + n + 1))
                    nc.scalar.activation(prob[n][:, :], prob[n][:, :], ACT.Exp, bias=neg_max[:, n:n + 1],
                                         accum_out=row_sum[:, n:n + 1]).then_inc(p_ready, 1)
                if what == "Q":
                    q_high(b, g + 1)
                if what == "swap":
                    k_exchange(kn + n, s)
                if what == "K":
                    k_high(kn + n, s, n)
                if what == "V":
                    v_high(sv_item(b, g, SCORES + v_fill(g, n)), n)
                if what == "C":
                    c_high(next_c_item(b), n)
                if what == "T":
                    act.wait_ge(t_ready, t_item(b, g, n, last) + 1)
                    nc.scalar.activation(pT[0][:, n % PT_SLOTS, :], t_banks[0:ST, n % 2, 0:2 * GQ], ACT.Copy).then_inc(t_hi, 1)

        with act.Fori(0, B - 1) as b:
            for g in range(HKV):
                step(b, g, False)
        for g in range(HKV):
            step(B - 1, g, True)

    @block.tensor
    def _(pe):
        def k_part(item, s, g, c, d, context_items):
            if d == 0:
                pe.wait_ge(k_free, item + 1)
                if context_items is not None:
                    pe.wait_ge(t_free, context_items + (RING + (c + 1) * CT))
            for n, (a, m) in enumerate(PASSES):
                mm = nc.tensor.matmul(k_banks[:, s, 0:SC], w[0][a][:, d, g * DH:(g + 1) * DH],
                                      cT[m][:, d, c * SC:(c + 1) * SC], start=(d == 0 and n == 0),
                                      stop=(d == DC - 1 and n == len(PASSES) - 1))
            if d == DC - 1:
                mm.then_inc(k_ready, 1)

        def v_part(item, g, m, t):
            if t == 0:
                pe.wait_ge(sv_free, item + 1)
            tile = 2 * m + t
            for d in range(DC):
                for n, (a, mv) in enumerate(PASSES):
                    mm = nc.tensor.matmul(sv_banks[0:ST, m % 2, t * PAIR:(t + 1) * PAIR],
                                          cT[a][:, d, tile * ST:(tile + 1) * ST], w[1][mv][:, d, g * DH:g * DH + PAIR],
                                          start=(d == 0 and n == 0), stop=(d == DC - 1 and n == len(PASSES) - 1))
            if t == 1:
                mm.then_inc(sv_ready, 1)

        def c_transposes(b, first, m):
            pe.wait_ge(t_free, first + (m + 1))
            if m % STAGE == 0:
                c_stage_ready(pe, b, m)
            for d in range(DC):
                mm = nc.tensor.transpose(t_banks[:, m % 2, d * ST:(d + 1) * ST], c_tile(m)[:, d * P:(d + 1) * P],
                                         ident[0:ST, 0:ST])
            mm.then_inc(t_ready, 1)

        def scores(b, g, i):
            h, c = divmod(i, NC)
            if i == 0:
                pe.wait_ge(q_lo, b * HKV + (g + 1))
            pe.wait_ge(sv_free, sv_item(b, g, i) + 1)
            if h == 0:
                pe.wait_ge(k_lo, k_item(b, g, c) + 1)
            for n, (a, m) in enumerate(PASSES):
                mm = nc.tensor.matmul(sv_banks[0:ROWS, i % 2, 0:SC], q[a][:, h * ROWS:(h + 1) * ROWS],
                                      k[m][:, c * SC:(c + 1) * SC], start=(n == 0), stop=(n == len(PASSES) - 1))
            mm.then_inc(sv_ready, 1)

        def transposes(b, g, j, last):
            pe.wait_ge(t_free, t_item(b, g, j, last) + 1)
            if j == 0:
                pe.wait_ge(p_ready, b * (HKV * HALVES) + (g + 1) * HALVES)
            for t in range(2):
                for h in range(HALVES):
                    col = t * GQ + h * ROWS
                    mm = nc.tensor.transpose(t_banks[0:ST, j % 2, col:col + ROWS],
                                             prob[h][:, (2 * j + t) * ST:(2 * j + t + 1) * ST], ident[0:ROWS, 0:ROWS])
            mm.then_inc(t_ready, 1)

        def spread_inv(b, g):
            pe.wait_ge(o_free, b * HKV + (g + 1))
            pe.wait_ge(inv_ready, b * (HKV * HALVES) + (g + 1) * HALVES)
            for h in range(HALVES):
                nc.tensor.transpose(o_banks[:, g % 2, GQ + h * ROWS:GQ + (h + 1) * ROWS],
                                    inv_sum[:, h:h + 1].broadcast_to([ROWS, P]), ident[0:ROWS, 0:ROWS])

        def weigh(b, g, j, last):
            pe.wait_ge(t_free, t_item(b, g, j, last) + (RING + 1))
            if g % 2 == 0 and j >= V_AHEAD:
                pe.wait_ge(sv_free, sv_item(b, g, SCORES + v_fill(g, j)) + (RING + 1))
            for t in range(2):
                for n, (a, m) in enumerate(PASSES):
                    mm = nc.tensor.matmul(o_banks[:, g % 2, 0:GQ], v[a][:, 2 * j + t, (g % 2) * DH:(g % 2 + 1) * DH],
                                          pT[m][:, j % PT_SLOTS, t * GQ:(t + 1) * GQ],
                                          start=(j == 0 and t == 0 and n == 0),
                                          stop=(j == PT - 1 and t == 1 and n == len(PASSES) - 1))
            if j == PT - 1:
                mm.then_inc(o_ready, 1)

        pe.wait_ge(w_lo, W_PIECES)
        for what, n in tasks(PE_STEP["first"]):
            if what == "C":
                c_transposes(0, 0, *n)
            if what == "K":
                k_part(n[0], n[0] % 2, 0, *n, 0)
            if what == "V":
                v_part(n[0], 0, *n)

        def step(b, g, last):
            kind = step_kind(g, last)
            for what, n in tasks(PE_STEP[kind]):
                if what == "S":
                    scores(b, g, *n)
                if what == "K":
                    k_part(k_item(b, g + 1, n[0]), ((g + 1) * NC + n[0]) % 2, (g + 1) % HKV, *n,
                           next_c_item(b) if kind == "turn" else None)
                if what == "V":
                    v_part(sv_item(b, g, SCORES + v_fill(g, n[0])), (g + g % 2) % HKV, *n)
                if what == "C":
                    c_transposes(b + 1, next_c_item(b), *n)
                if what == "T":
                    transposes(b, g, *n, last)
                if what == "inv":
                    spread_inv(b, g)
                if what == "PV":
                    weigh(b, g, *n, last)

        with pe.Fori(0, B - 1) as b:
            for g in range(HKV):
                step(b, g, False)
        for g in range(HKV):
            step(B - 1, g, True)

    @block.vector
    def _(dve):
        for ring in (k_free, sv_free, t_free, o_free):
            dve.sem_inc(ring, RING)

        def k_cos_part(item, s, c):
            dve.wait_ge(k_swapped, item * 2 + 2)
            if not isinstance(item, int) or item >= 2:
                dve.wait_ge(k_lo, item - 1)
            nc.vector.tensor_tensor(k_rot[:, s], k_banks[:, s, 0:SC], cos_t[:, c * SC:(c + 1) * SC],
                                    ALU.mult).then_inc(k_free, 1)

        def k_rotate(item, s, c):
            nc.vector.tensor_tensor(k_swap[:, s], k_swap[:, s], sin_t[:, c * SC:(c + 1) * SC],
                                    ALU.mult).then_inc(k_sined, 1)
            dve.wait_ge(k_free, item + (RING + 1))
            dve.wait_ge(k_sined, item + 1)
            nc.vector.tensor_tensor(k_rot[:, s], k_rot[:, s], k_swap[:, s], ALU.add).then_inc(k_rotated, 1)

        def c_low(item, m):
            dve.wait_ge(t_hi, item + m + 1)
            dst = slice(m * ST, (m + 1) * ST)
            nc.vector.tensor_tensor(cT[1][:, :, dst], t_banks[:, m % 2, 0:DC * ST].rearrange("p (c s) -> p c s", c=DC),
                                    f32(cT[0][:, :, dst]), ALU.subtract).then_inc(t_free, 1)

        def q_low(b, g):
            dve.wait_ge(q_hi, b * HKV + (g + 1))
            nc.vector.tensor_tensor(q[1][:, :], q_raw[:, g % 2], f32(q[0][:, :]), ALU.subtract).then_inc(q_lo, 1)

        def v_low(item, m):
            dve.wait_ge(v_hi, item + 1)
            nc.vector.tensor_tensor(v[1][:, 2 * m:2 * m + 2, :], sv_banks[0:ST, m % 2, :].rearrange("p (t n) -> p t n", t=2),
                                    f32(v[0][:, 2 * m:2 * m + 2, :]), ALU.subtract).then_inc(sv_free, 1)

        for n in range(W_PIECES):
            dve.wait_ge(w_hi, n + 1)
            nc.vector.tensor_tensor(w[n // DC][1][:, n % DC, :], stage[:, n % 2, 0:HKV * DH],
                                    f32(w[n // DC][0][:, n % DC, :]), ALU.subtract).then_inc(w_lo, 1)
        dve.wait_ge(tables_loaded, 32)
        for what, (n, *_) in tasks(DVE_STEP["first"]):
            if what == "Q":
                q_low(0, 0)
            if what == "C":
                c_low(0, n)
            if what == "cos":
                k_cos_part(n, n % 2, n)
            if what == "rot":
                k_rotate(n, n % 2, n)
            if what == "V":
                v_low(n, n)

        def step(b, g, last):
            kn = k_item(b, g + 1)
            if g == 0:
                dve.wait_ge(mask_loaded, b * 32 + 32)
            for what, (n, *_) in tasks(DVE_STEP[step_kind(g, last)]):
                s = ((g + 1) * NC + n) % 2
                if what == "mask":
                    h, c = divmod(n, NC)
                    wait_apart(dve, sv_ready, sv_item(b, g, n) + 1, dve_passed)
                    nc.vector.tensor_tensor_reduce(prob[h][:, c * SC:(c + 1) * SC], sv_banks[0:ROWS, n % 2, 0:SC],
                                                   mask_t[:, c * SC:(c + 1) * SC], 1.0, LOWEST, ALU.add, ALU.max,
                                                   chunk_max[:, h, c:c + 1]).then_inc(sv_free, 1)
                if what == "max":
                    dve.wait_ge(sv_free, sv_item(b, g, (n + 1) * NC) + RING)
                    nc.vector.tensor_reduce(neg_max[:, n:n + 1], chunk_max[:, n, :], AX_X, ALU.max,
                                            negate=True).then_inc(max_ready, 1)
                if what == "inv":
                    for h in range(HALVES):
                        dve.wait_ge(p_ready, b * (HKV * HALVES) + (g * HALVES + h + 1))
                        nc.vector.reciprocal(inv_sum[:, h:h + 1], row_sum[:, h:h + 1]).then_inc(inv_ready, 1)
                if what == "Q":
                    q_low(b, g + 1)
                if what == "cos":
                    k_cos_part(kn + n, s, n)
                if what == "rot":
                    k_rotate(kn + n, s, n)
                if what == "V":
                    v_low(b * (HKV // 2 * VT) + (V_AHEAD + g // 2 * VT + (g % 2) * V_REST + v_fill(g, n)), n)
                if what == "C":
                    c_low(next_c_item(b), n)
                if what == "T":
                    dve.wait_ge(t_hi, t_item(b, g, n, last) + 1)
                    nc.vector.tensor_tensor(pT[1][:, n % PT_SLOTS, :], t_banks[0:ST, n % 2, 0:2 * GQ],
                                            f32(pT[0][:, n % PT_SLOTS, :]), ALU.subtract).then_inc(t_free, 1)
                if what == "out":
                    dve.wait_ge(o_ready, b * HKV + (g + 1))
                    dve.wait_ge(o_free, b * HKV + (RING + g))
                    nc.vector.tensor_copy(inv_b[:, :], o_banks[:, g % 2, GQ:2 * GQ]).then_inc(inv_copied, 1)
                    dve.wait_ge(inv_copied, b * HKV + (g + 1))
                    dve.wait_ge(attn_stored[g % 2], b * (16 * steps2) + 16 * (g // 2 + 1))
                    nc.vector.tensor_tensor(attn[:, g % 2], o_banks[:, g % 2, 0:GQ], inv_b[:, :], ALU.mult).then_inc(o_free, 1)

        with dve.Fori(0, B - 1) as b:
            for g in range(HKV):
                step(b, g, False)
        for g in range(HKV):
            step(B - 1, g, True)


def output_part(nc, ctx, ident, x, wo, a_in, b_in, wr, g_xattn, g_ffn, attn_dram, out):
    def sb(name, shape, dt=F32):
        return ctx.enter_context(nc.sbuf_tensor(name, shape, dt))

    def sem(name):
        return ctx.enter_context(nc.semaphore(name))

    attn_raw = sb("attn_raw", [P, 2, B, REP, SQ])
    attn_s = [sb(f"attn_{n}", [P, 2, REP, B, SQ], F32R) for n in ("hi", "lo")]
    wo_raw = sb("wo_raw", [P, 2, REP, D])
    wo_s = [sb(f"wo_{n}", [P, 2, REP, D], F32R) for n in ("hi", "lo")]
    x_tok = sb("o_x_tok", [ROWS, NTT, D])
    y = sb("y", [ROWS, NTT, D])
    yn = sb("yn", [ROWS, NTT, D])
    res = sb("res", [ROWS, NTT, D])
    gate_raw = sb("gate_raw", [ROWS, 2])
    tanh_g = sb("tanh_g", [ROWS, 2])
    ar = sb("ar", [ER + EXPERTS, D])
    arT = sb("arT", [P, DC, ER + EXPERTS])
    b_raw = sb("b_raw", [P, DC, EXPERTS, RANK])
    bT = sb("bT", [ER, D])
    stats = sb("o_stats", [ROWS, NTT, 6])
    mv = sb("o_mv", [ROWS, NTT, 2])
    var = sb("o_var", [ROWS, NTT])
    std = sb("o_std", [ROWS, NTT])
    rstd = sb("o_rstd", [ROWS, NTT])
    yT = sb("yT", [P, DC, TOK])
    z = sb("z", [ROWS, NTT, ER + EXPERTS])
    earlier = sb("earlier", [ROWS, NTT, EXPERTS, EXPERTS])
    beats = sb("beats", [ROWS, NTT, EXPERTS, EXPERTS])
    ties = sb("ties", [ROWS, NTT, EXPERTS, EXPERTS])
    rank = sb("rank", [ROWS, NTT, EXPERTS])
    top = sb("top", [ROWS, NTT])
    shifted = sb("shifted", [ROWS, NTT, EXPERTS])
    gates = sb("gates", [ROWS, NTT, EXPERTS])
    total = sb("total", [ROWS, NTT])
    inv_total = sb("inv_total", [ROWS, NTT])
    mid = sb("mid", [ROWS, NTT, EXPERTS, RANK])
    midT = sb("midT", [ER, TOK])
    acc = ctx.enter_context(nc.psum_tensor("acc", [P, NTT, BANK], F32))
    yT_banks = ctx.enter_context(nc.psum_tensor("yT_banks", [P, DC, BANK], F32))

    attn_loaded = [sem(f"attn_loaded{i}") for i in range(2)]
    wo_loaded = [sem(f"wo_loaded{i}") for i in range(2)]
    sp_passed = sem("o_sp_passed")
    x_loaded, small_loaded = sem("o_x_loaded"), sem("small_loaded")
    attn_hi, attn_lo, wo_hi, wo_lo = sem("attn_hi_ready"), sem("attn_lo_ready"), sem("wo_hi_ready"), sem("wo_lo_ready")
    group_done, tanh_ready, y_ready = sem("group_done"), sem("tanh_ready"), sem("y_ready")
    stats_ready, mv_ready, var_ready, std_ready, rstd_ready, yn_ready = (
        sem(f"o_{n}_ready") for n in ("stats", "mv", "var", "std", "rstd", "yn"))
    small_banked, small_copied = sem("small_banked"), sem("small_copied")
    yT_banked, yT_ready, z_banked, z_ready = sem("yT_banked"), sem("yT_ready"), sem("z_banked"), sem("z_ready")
    gate_steps, earlier_steps, exp_ready, mid_ready = sem("gate_steps"), sem("earlier_steps"), sem("exp_ready"), sem("mid_ready")
    midT_banked, midT_ready, delta_ready, res_ready, stored = (
        sem(n) for n in ("midT_banked", "midT_ready", "delta_ready", "res_ready", "stored"))

    x_v = x.rearrange("(t b) s d -> (b s) t d", t=NTT)
    out_v = out.rearrange("(t b) s d -> (b s) t d", t=NTT)
    wo_v = wo.rearrange("(g h p) n -> g p h n", h=REP, p=P)
    pairs = HKV // 2
    SMALL = 16 * (4 + DC)

    block = ctx.enter_context(nc.Block())

    @block.sync
    def _(sp):
        def load_group(g, u):
            sp.dma_start(attn_raw[:, u].rearrange("p b h s -> p (b h s)"),
                         attn_dram[bass.ds(g, 1)].rearrange("g p b n -> p (g b n)")).then_inc(attn_loaded[u], 16)
            sp.dma_start(wo_raw[:, u], wo_v[bass.ds(g, 1)].rearrange("g p h n -> p (g h) n")).then_inc(wo_loaded[u], 16)

        load_group(0, 0)
        load_group(1, 1)
        sp.dma_start(x_tok[:, :, :], x_v).then_inc(x_loaded, 16)
        with nc.allow_non_contiguous_dma("small operands"):
            sp.dma_start(ar[0:ER, :], a_in.rearrange("e r f -> (e r) f")).then_inc(small_loaded, 16)
            sp.dma_start(ar[ER:ER + EXPERTS, :], wr).then_inc(small_loaded, 16)
            for n, gate in enumerate((g_xattn, g_ffn)):
                sp.dma_start(gate_raw[:, n:n + 1], gate.rearrange("(a n) -> a n", a=1).broadcast_to([ROWS, 1])).then_inc(small_loaded, 16)
            for c in range(DC):
                sp.dma_start(b_raw[:, c], b_in[:, c * P:(c + 1) * P, :].rearrange("e o r -> o e r")).then_inc(small_loaded, 16)

        def two_groups(i):
            for u in range(2):
                sp.wait_ge(attn_lo, i * 2 + (u + 1))
                wait_apart(sp, wo_lo, i * 2 + (u + 1), sp_passed)
                load_group(i * 2 + (2 + u), u)

        with sp.Fori(0, pairs - 1) as i:
            two_groups(i)
        for t in range(NTT):
            sp.wait_ge(res_ready, t + 1)
            sp.dma_start(out_v[:, t], res[:, t]).then_inc(stored, 16)
        sp.wait_ge(stored, 16 * NTT)

    @block.gpsimd
    def _(pool):
        nc.gpsimd.memset(earlier[:, :, :, :], 1.0).then_inc(earlier_steps, 1)
        pool.wait_ge(earlier_steps, 1)
        nc.gpsimd.affine_select(out=earlier[:, :, :, :], in_=earlier[:, :, :, :], compare_op=ALU.is_gt, fill=0.0, base=0,
                                pattern=[[0, NTT], [1, EXPERTS], [-1, EXPERTS]], channel_multiplier=0).then_inc(earlier_steps, 1)

    @block.scalar
    def _(act):
        def split_group(n, u, needs_use):
            act.wait_ge(attn_loaded[u], (n - u) * 8 + 16)
            if needs_use:
                act.wait_ge(group_done, n - 1)
            nc.scalar.activation(attn_s[0][:, u].rearrange("p h b s -> p b h s"), attn_raw[:, u], ACT.Copy).then_inc(attn_hi, 1)
            act.wait_ge(wo_loaded[u], (n - u) * 8 + 16)
            nc.scalar.activation(wo_s[0][:, u], wo_raw[:, u], ACT.Copy).then_inc(wo_hi, 1)

        for u in range(2):
            split_group(u, u, False)
        with act.Fori(1, pairs) as i:
            for u in range(2):
                split_group(i * 2 + u, u, True)
        act.wait_ge(small_loaded, SMALL)
        nc.scalar.activation(tanh_g[:, :], gate_raw[:, :], ACT.Tanh).then_inc(tanh_ready, 1)
        act.wait_ge(var_ready, 1)
        nc.scalar.activation(std[:, :], var[:, :], ACT.Sqrt).then_inc(std_ready, 1)
        for c in range(0, DC, 2):
            act.wait_ge(yT_banked, c + 1)
            nc.scalar.activation(yT[:, c, :], yT_banks[:, c, 0:TOK], ACT.Copy).then_inc(yT_ready, 1)
        act.wait_ge(gate_steps, 4)
        nc.scalar.activation(gates[:, :, :], shifted[:, :, :], ACT.Exp).then_inc(exp_ready, 1)

    @block.tensor
    def _(pe):
        def group(g, u, first, last):
            pe.wait_ge(attn_lo, g + 1)
            pe.wait_ge(wo_lo, g + 1)
            for h in range(REP):
                for t in range(NTT):
                    for n, (a, m) in enumerate(PASSES):
                        mm = nc.tensor.matmul(acc[0:ROWS, t, :],
                                              attn_s[a][:, u, h].rearrange("p b s -> p (b s)")[:, t * ROWS:(t + 1) * ROWS],
                                              wo_s[m][:, u, h, :], start=(first and h == 0 and n == 0),
                                              stop=(last and h == REP - 1 and n == len(PASSES) - 1), skip_group_check=True)
            mm.then_inc(group_done, 1)

        group(0, 0, True, False)
        group(1, 1, False, False)
        with pe.Fori(1, pairs - 1) as i:
            for u in range(2):
                group(i * 2 + u, u, False, False)
        group(HKV - 2, 0, False, False)
        group(HKV - 1, 1, False, True)

        pe.wait_ge(small_loaded, SMALL)
        n = ER + EXPERTS
        for c in range(DC):
            mm = nc.tensor.transpose(yT_banks[:, 0, c * n:(c + 1) * n], ar[:, c * P:(c + 1) * P], ident[0:n, 0:n])
        mm.then_inc(small_banked, 1)
        for c in range(DC):
            mm = nc.tensor.transpose(yT_banks[0:ER, 1, c * P:(c + 1) * P], b_raw[:, c].rearrange("p e r -> p (e r)"), ident[:, :])
        mm.then_inc(small_banked, 1)
        pe.wait_ge(small_copied, 2)
        for c in range(DC):
            for t in range(NTT):
                if c == 0:
                    pe.wait_ge(yn_ready, t + 1)
                mm = nc.tensor.transpose(yT_banks[:, c, t * ROWS:(t + 1) * ROWS], yn[:, t, c * P:(c + 1) * P], ident[0:ROWS, 0:ROWS])
            mm.then_inc(yT_banked, 1)
        pe.wait_ge(yT_ready, DC)
        for t in range(NTT):
            for c in range(DC):
                mm = nc.tensor.matmul(acc[0:ROWS, 0, t * n:(t + 1) * n], yT[:, c, t * ROWS:(t + 1) * ROWS], arT[:, c, :],
                                      start=(c == 0), stop=(c == DC - 1))
        mm.then_inc(z_banked, 1)
        pe.wait_ge(mid_ready, 1)
        for t in range(NTT):
            mm = nc.tensor.transpose(yT_banks[0:ER, 0, t * ROWS:(t + 1) * ROWS], mid[:, t].rearrange("p e r -> p (e r)"), ident[0:ROWS, 0:ROWS])
        mm.then_inc(midT_banked, 1)
        pe.wait_ge(midT_ready, 1)
        for t in range(NTT):
            nc.tensor.matmul(acc[0:ROWS, t, :], midT[:, t * ROWS:(t + 1) * ROWS], bT[:, :], start=True, stop=True).then_inc(delta_ready, 1)

    @block.vector
    def _(dve):
        def split_group(n, u):
            dve.wait_ge(attn_hi, n + 1)
            nc.vector.tensor_tensor(attn_s[1][:, u].rearrange("p h b s -> p b h s"), attn_raw[:, u],
                                    f32(attn_s[0][:, u]).rearrange("p h b s -> p b h s"), ALU.subtract).then_inc(attn_lo, 1)
            dve.wait_ge(wo_hi, n + 1)
            nc.vector.tensor_tensor(wo_s[1][:, u], wo_raw[:, u], f32(wo_s[0][:, u]), ALU.subtract).then_inc(wo_lo, 1)

        with dve.Fori(0, pairs) as i:
            for u in range(2):
                split_group(i * 2 + u, u)
        dve.wait_ge(small_banked, 1)
        nc.vector.tensor_copy(arT[:, :, :], yT_banks[:, 0, 0:DC * (ER + EXPERTS)].rearrange("p (c n) -> p c n", c=DC)).then_inc(small_copied, 1)
        dve.wait_ge(small_banked, 2)
        nc.vector.tensor_copy(bT[:, :], yT_banks[0:ER, 1, :]).then_inc(small_copied, 1)
        dve.wait_ge(x_loaded, 16)
        dve.wait_ge(tanh_ready, 1)
        dve.wait_ge(group_done, HKV)
        for t in range(NTT):
            nc.vector.scalar_tensor_tensor(out=y[:, t], in0=acc[0:ROWS, t, :], scalar=tanh_g[:, 0:1], in1=x_tok[:, t],
                                           op0=ALU.mult, op1=ALU.add).then_inc(y_ready, 1)
        for t in range(NTT):
            dve.wait_ge(y_ready, t + 1)
            nc.vector.bn_stats(stats[:, t], y[:, t]).then_inc(stats_ready, 1)
        for t in range(NTT):
            dve.wait_ge(stats_ready, t + 1)
            nc.vector.bn_aggr(mv[:, t], stats[:, t]).then_inc(mv_ready, 1)
        dve.wait_ge(mv_ready, NTT)
        nc.vector.tensor_scalar(var[:, :], mv[:, :, 1], EPS, None, ALU.add).then_inc(var_ready, 1)
        dve.wait_ge(std_ready, 1)
        nc.vector.reciprocal(rstd[:, :], std[:, :]).then_inc(rstd_ready, 1)
        dve.wait_ge(rstd_ready, 1)
        for t in range(NTT):
            nc.vector.tensor_scalar(yn[:, t], y[:, t], mv[:, t, 0:1], rstd[:, t:t + 1], ALU.subtract, ALU.mult).then_inc(yn_ready, 1)
        for c in range(1, DC, 2):
            dve.wait_ge(yT_banked, c + 1)
            nc.vector.tensor_copy(yT[:, c, :], yT_banks[:, c, 0:TOK]).then_inc(yT_ready, 1)
        dve.wait_ge(z_banked, 1)
        nc.vector.tensor_copy(z[:, :, :], acc[0:ROWS, 0, 0:NTT * (ER + EXPERTS)].rearrange("p (t n) -> p t n", t=NTT)).then_inc(z_ready, 1)
        dve.wait_ge(z_ready, 1)
        logits = z[:, :, ER:ER + EXPERTS]
        square = [ROWS, NTT, EXPERTS, EXPERTS]
        of_e = logits[:, :, :, None].broadcast_to(square)
        of_j = logits[:, :, None, :].broadcast_to(square)
        nc.vector.tensor_reduce(top[:, :], logits, AX_X, ALU.max).then_inc(gate_steps, 1)
        nc.vector.tensor_tensor(beats[:, :, :, :], of_j, of_e, ALU.is_gt).then_inc(gate_steps, 1)
        nc.vector.tensor_tensor(ties[:, :, :, :], of_j, of_e, ALU.is_equal).then_inc(gate_steps, 1)
        dve.wait_ge(gate_steps, 3)
        nc.vector.tensor_tensor(shifted[:, :, :], logits, top[:, :, None].broadcast_to([ROWS, NTT, EXPERTS]), ALU.subtract).then_inc(gate_steps, 1)
        dve.wait_ge(earlier_steps, 2)
        nc.vector.tensor_tensor(ties[:, :, :, :], ties[:, :, :, :], earlier[:, :, :, :], ALU.mult).then_inc(gate_steps, 1)
        dve.wait_ge(gate_steps, 5)
        nc.vector.tensor_tensor(beats[:, :, :, :], beats[:, :, :, :], ties[:, :, :, :], ALU.add).then_inc(gate_steps, 1)
        dve.wait_ge(gate_steps, 6)
        nc.vector.tensor_reduce(rank[:, :, :], beats[:, :, :, :], AX_X, ALU.add).then_inc(gate_steps, 1)
        dve.wait_ge(gate_steps, 7)
        nc.vector.tensor_scalar(rank[:, :, :], rank[:, :, :], 2.0, None, ALU.is_lt).then_inc(gate_steps, 1)
        dve.wait_ge(gate_steps, 8)
        dve.wait_ge(exp_ready, 1)
        nc.vector.tensor_tensor(gates[:, :, :], gates[:, :, :], rank[:, :, :], ALU.mult).then_inc(gate_steps, 1)
        dve.wait_ge(gate_steps, 9)
        nc.vector.tensor_reduce(total[:, :], gates[:, :, :], AX_X, ALU.add).then_inc(gate_steps, 1)
        dve.wait_ge(gate_steps, 10)
        nc.vector.reciprocal(inv_total[:, :], total[:, :]).then_inc(gate_steps, 1)
        dve.wait_ge(gate_steps, 11)
        nc.vector.tensor_tensor(gates[:, :, :], gates[:, :, :], inv_total[:, :, None].broadcast_to([ROWS, NTT, EXPERTS]), ALU.mult).then_inc(gate_steps, 1)
        dve.wait_ge(gate_steps, 12)
        nc.vector.tensor_scalar(gates[:, :, :], gates[:, :, :], LORA_SCALE, None, ALU.mult).then_inc(gate_steps, 1)
        dve.wait_ge(gate_steps, 13)
        for t in range(NTT):
            mm = nc.vector.tensor_tensor(mid[:, t], z[:, t, 0:ER].rearrange("p (e r) -> p e r", e=EXPERTS),
                                         gates[:, t, :, None].broadcast_to([ROWS, EXPERTS, RANK]), ALU.mult)
        mm.then_inc(mid_ready, 1)
        dve.wait_ge(midT_banked, 1)
        nc.vector.tensor_copy(midT[:, :], yT_banks[0:ER, 0, 0:TOK]).then_inc(midT_ready, 1)
        for t in range(NTT):
            dve.wait_ge(delta_ready, t + 1)
            nc.vector.scalar_tensor_tensor(out=res[:, t], in0=acc[0:ROWS, t, :], scalar=tanh_g[:, 1:2], in1=y[:, t],
                                           op0=ALU.mult, op1=ALU.add).then_inc(res_ready, 1)


def flamingo_block(nc, x, ctx_in, mask, g_xattn, g_ffn, wq, wk, wv, wo, a_in, b_in, wr,
                   q_cos, q_sin, k_cos, k_sin, out):
    q_dram = nc.dram_tensor("q_by_head", (HKV, P, B, GQ), F32).ap()
    attn_dram = nc.dram_tensor("attn_by_head", (HKV, P, B, GQ), F32).ap()
    with ExitStack() as whole:
        ident = whole.enter_context(nc.sbuf_tensor("ident", [P, P], F32))
        with ExitStack() as ctx:
            query_part(nc, ctx, ident, x, wq, q_cos, q_sin, q_dram)
        with ExitStack() as ctx:
            attention_part(nc, ctx, ident, ctx_in, mask, wk, wv, k_cos, k_sin, q_dram, attn_dram)
        with ExitStack() as ctx:
            output_part(nc, ctx, ident, x, wo, a_in, b_in, wr, g_xattn, g_ffn, attn_dram, out)


def rotary_tables(positions, scale):
    inv_freq = (1.0 / np.float32(10000.0) ** (np.arange(0, DH, 2, dtype=np.float32) / np.float32(DH))).astype(np.float32)
    ang = (inv_freq[:, None] * np.arange(positions, dtype=np.float32)[None, :]).astype(np.float32)
    cos, sin = np.cos(ang).astype(np.float32), np.sin(ang).astype(np.float32)
    return (np.concatenate([cos, cos]) * np.float32(scale)).astype(np.float32), \
        (np.concatenate([-sin, sin]) * np.float32(scale)).astype(np.float32)


_INS = ['x', 'ctx_4096', 'mask_BxSxS2_ff0', 'g_xattn', 'g_ffn', 'L0_xattn_wq', 'L0_xattn_wk', 'L0_xattn_wv',
        'L0_xattn_wo', 'L0_ffn_A', 'L0_ffn_B', 'L0_ffn_Wr']
_OUTS = [((B, SQ, D), 'float32')]


def kernel(**inputs):
    import numpy as _np
    import concourse.bacc as _bacc
    from concourse import mybir as _mybir
    from concourse.bass_utils import run_bass_kernel_spmd as _run

    nc = _bacc.Bacc("TRN2", target_bir_lowering=False, num_devices=1, dynamic_dma_scratch_size=1024)
    given = {name: _np.ascontiguousarray(inputs[name]) for name in _INS}
    given["q_cos"], given["q_sin"] = rotary_tables(SQ, 1.0 / _np.sqrt(_np.float32(DH)))
    given["k_cos"], given["k_sin"] = rotary_tables(SK, 1.0)
    arrays, args = {}, []
    for name, a in given.items():
        arrays[f"in_{name}_dram"] = a
        args.append(nc.dram_tensor(f"in_{name}_dram", a.shape, _mybir.dt.from_np(a.dtype), kind="ExternalInput").ap())
    for i, (shape, dtype) in enumerate(_OUTS):
        dt = _mybir.dt.from_np(_np.dtype(dtype))
        args.append(nc.dram_tensor(f"out_{i}_dram", shape, dt, kind="ExternalOutput").ap())
    flamingo_block(nc, *args)
    r = _run(nc, [arrays], core_ids=[0])
    got = tuple(r.results[0][f"out_{i}_dram"] for i in range(len(_OUTS)))
    return got[0]
```

```python
from contextlib import ExitStack

import numpy as np

import concourse.bass as bass
from concourse import mybir
from concourse.alu_op_type import AluOpType as ALU

ACT = mybir.ActivationFunctionType
F32 = mybir.dt.float32
F32R = mybir.dt.float32r
AX_X = mybir.AxisListType.X

P = 128
B, SQ, D = 8, 56, 512
SK = 1500
HKV, REP, DH = 8, 4, 128
DC = D // P
HALF = DH // 2
TOK = B * SQ
ROWS = 2 * SQ
NTT = TOK // ROWS
HALVES = REP // 2
GQ = REP * SQ
GW = REP * DH
ST = 125
NT = SK // ST
SC = 500
NC = SK // SC
CT = SC // ST
PAIR = 2 * DH
VT = NT // 2
PT = NT // 2
STAGE = 3
STAGES = NT // STAGE
BANK = 512
RING = 2
PT_SLOTS = 3
EXPERTS, RANK = 4, 16
ER = EXPERTS * RANK
LORA_SCALE = 16.0 / float(np.sqrt(16.0))
EPS = 1e-5
LOWEST = -3.4e38
PASSES = ((0, 0), (1, 0), (0, 1))

V_AHEAD = 4
V_REST = VT - V_AHEAD
SCORES = HALVES * NC

K_ITEMS = HKV * NC
SV_ITEMS = HKV * SCORES + (HKV // 2) * VT
T_ITEMS = HKV * PT + NT

PE_STEP = {
    "even": ("K00 S0 S1 K01 K02 S2 S3 K03 K10 S4 S5 K11 K12 K13 V40 K20 T0 T1 K21 V41 K22 T2 K23 PV0 V50 T3 PV1 T4 "
             "V51 PV2 T5 PV3 PV4 PV5"),
    "odd": ("S0 S1 K00 K01 S2 S3 K02 K03 S4 S5 K10 K11 K12 K13 K20 K21 T0 K22 T1 K23 T2 PV0 V00 T3 V01 PV1 PV2 V10 "
            "T4 V11 PV3 V20 V21 T5 V30 V31 PV4 PV5"),
    "turn": ("C0 C1 S0 S1 C2 C3 S2 S3 C4 C5 K00 S4 K01 S5 C6 C7 K02 K03 C8 C9 K10 K11 C10 C11 K12 K13 T0 T1 K20 K21 "
             "K22 PV0 K23 T2 V00 T3 V01 PV1 T4 PV2 V10 PV3 V11 T5 V20 V21 V30 V31 PV4 PV5"),
    "last": "S0 S1 S2 S3 S4 S5 T0 T1 T2 PV0 T3 PV1 T4 PV2 T5 PV3 PV4 PV5",
    "first": ("C0 C1 C2 V00 C3 V01 C4 K00 C5 K01 K02 C6 K03 V10 C7 V11 C8 K10 C9 K11 C10 K12 C11 K13 V20 K20 K21 "
              "K22 K23 V21 V30 V31"),
}
ACT_STEP = {
    "even": "exp0 swap0 exp1 swap1 Q K0 T0 T1 V4 T2 swap2 T3 T4 V5 T5 K1 K2 out",
    "odd": "exp0 swap0 exp1 swap1 T0 T1 Q T2 T3 V0 T4 swap2 K0 V1 K1 T5 V2 V3 K2 out",
    "turn": ("C0 C1 C2 C3 C4 C5 exp0 C6 C7 exp1 C8 C9 swap0 C10 C11 T0 swap1 T1 Q T2 K0 T3 swap2 V0 T4 V1 V2 T5 K1 "
             "V3 K2 out"),
    "last": "wo0 exp0 exp1 attn0 T0 T1 T2 T3 T4 T5 out",
    "first": "C0 C1 C2 C3 V0 C4 C5 C6 swap0 C7 V1 C8 C9 K0 C10 C11 swap1 Q K1 swap2 V2 K2 V3",
}
DVE_STEP = {
    "even": ("mask0 mask1 mask2 mask3 max0 mask4 mask5 max1 cos0 sin0 rot0 cos1 T0 T1 sin1 rot1 T2 Q V4 inv cos2 T3 "
             "sin2 T4 rot2 V5 T5 out"),
    "odd": ("mask0 mask1 mask2 max0 mask3 mask4 mask5 max1 cos0 sin0 inv T0 rot0 T1 T2 cos1 V0 sin1 rot1 T3 T4 Q V1 "
            "cos2 T5 sin2 V2 rot2 V3 out"),
    "turn": ("C0 C1 mask0 mask1 C2 C3 mask2 mask3 max0 C4 C5 mask4 mask5 max1 C6 C7 C8 C9 cos0 C10 C11 T0 sin0 rot0 "
             "inv cos1 T1 T2 T3 T4 Q V0 sin1 cos2 V1 rot1 sin2 T5 rot2 V2 V3 out"),
    "last": "mask0 mask1 mask2 max0 mask3 mask4 mask5 max1 inv T0 T1 T2 T3 T4 T5 out",
    "first": "C0 C1 C2 C3 V0 C4 C5 C6 cos0 sin0 C7 V1 rot0 C8 C9 C10 C11 cos1 sin1 rot1 Q cos2 sin2 V2 rot2 V3",
}


def step_kind(g, last):
    return ("last" if last else "turn") if g == HKV - 1 else ("odd" if g % 2 else "even")


def tasks(order):
    for word in order.split():
        what = word.rstrip("0123456789")
        digits = word[len(what):]
        numbers = tuple(int(x) for x in digits) if what in ("K", "V") else (int(digits),) if digits else (0,)
        yield what, numbers


def t_fills(table, kind):
    return [(what, n) for what, (n, *_) in tasks(table[kind]) if what in ("C", "T")]


def t_place(kind, what, n):
    fills = t_fills(PE_STEP, kind)
    assert fills == t_fills(ACT_STEP, kind) == t_fills(DVE_STEP, kind)
    return fills.index((what, n))


def f32(ap):
    return ap.bitcast(F32)


def k_item(b, g, c=0):
    return b * K_ITEMS + g * NC + c


def sv_item(b, g, i=0):
    return b * SV_ITEMS + (V_AHEAD + (g // 2) * (2 * SCORES + VT) + (g % 2) * (SCORES + V_REST) + i)


def v_fill(g, m):
    return m - (0 if g % 2 else V_AHEAD)


def t_item(b, g, j, last):
    return b * T_ITEMS + (NT + g * PT + t_place(step_kind(g, last), "T", j))


def c_item(b, m):
    return b * T_ITEMS + (NT + (HKV - 1) * PT + t_place("turn", "C", m))


def wait_apart(eng, sem, value, passed):
    eng.wait_ge(sem, value)
    eng.sem_inc(passed, 1)


class Shared:

    def __init__(self, nc, ctx):
        def sb(name, shape, dt=F32):
            return ctx.enter_context(nc.sbuf_tensor(name, shape, dt))

        def sem(name):
            return ctx.enter_context(nc.semaphore(name))

        self.ident = sb("ident", [P, P])
        self.w = [[sb(f"{n}_{h}", [P, DC, HKV * DH], F32R) for h in ("hi", "lo")] for n in ("wk", "wv")]
        self.stage = sb("stage", [P, 2, STAGE * D])
        self.tables = sb("k_tables", [P, 2, SK])
        self.mask_t = sb("mask_t", [ROWS, SK])
        self.head_rows = sb("head_rows", [P, B, REP, SQ])
        self.k_work = sb("k_work", [P, max(4 * SC, REP * D)])
        self.attn = sb("attn", [P, 2, GQ])
        self.stage_loaded = [sem(f"stage_loaded{i}") for i in range(2)]
        self.tables_loaded, self.mask_loaded = sem("k_tables_loaded"), sem("mask_loaded")
        self.w_hi, self.w_lo = sem("w_hi_ready"), sem("w_lo_ready")
        self.q_stored = [sem(f"q_stored{i}") for i in range(2)]
        self.attn_stored = [sem(f"attn_stored{i}") for i in range(2)]
        self.attn_loaded = [sem(f"attn_loaded{i}") for i in range(2)]
        self.wo_loaded = [sem(f"wo_loaded{i}") for i in range(2)]
        self.attn_hi, self.attn_lo, self.wo_hi, self.wo_lo = (
            sem(n) for n in ("attn_hi_ready", "attn_lo_ready", "wo_hi_ready", "wo_lo_ready"))

    def output_operands(self, context_halves):
        heads = dict(u=2, h=REP)
        self.attn_s = [half[:, :, :].rearrange("p c s -> p (c s)")[:, 0:2 * REP * TOK].rearrange(
            "p (u h b s) -> p u h b s", b=B, **heads) for half in context_halves]
        self.wo_s = [half[:, :, :].rearrange("p c n -> p (c n)").rearrange("p (u h n) -> p u h n", **heads)
                     for half in self.w[0]]
        self.wo_raw = [flat[:, 0:REP * D].rearrange("p (h n) -> p h n", h=REP)
                       for flat in (self.stage[:, :, :].rearrange("p u n -> p (u n)"), self.k_work[:, :])]
        self.attn_raw = [self.tables[:, :, :].rearrange("p u n -> p (u n)")[:, 0:REP * TOK].rearrange(
            "p (b h s) -> p b h s", b=B, h=REP), self.head_rows[:, :, :, :]]


def context_views(ctx_in):
    return ctx_in.rearrange("b (k t p) d -> b k p t d", k=STAGES, p=ST)


def load_context(nc, sp, shared, ctx_v, b, n):
    sp.dma_start(shared.stage[0:ST, n % 2].rearrange("p (t d) -> p t d", t=STAGE),
                 ctx_v[bass.ds(b, 1), n].rearrange("b p t d -> p (b t) d")).then_inc(shared.stage_loaded[n % 2], 16)


def load_mask(sp, shared, mask, b):
    for r in range(2):
        sp.dma_start(shared.mask_t[r * SQ:(r + 1) * SQ, :],
                     mask[bass.ds(b, 1)].rearrange("b s n -> (b s) n")).then_inc(shared.mask_loaded, 16)


def load_wo(sp, shared, wo, g, u):
    sp.dma_start(shared.wo_raw[u], wo.rearrange("(g h p) n -> g p h n", h=REP, p=P)[bass.ds(g, 1)].rearrange(
        "g p h n -> p (g h) n")).then_inc(shared.wo_loaded[u], 16)


def load_attn(sp, shared, attn_dram, g, u):
    sp.dma_start(shared.attn_raw[u].rearrange("p b h s -> p (b h s)"),
                 attn_dram[bass.ds(g, 1)].rearrange("g p b n -> p (g b n)")).then_inc(shared.attn_loaded[u], 16)


def query_part(nc, ctx, shared, x, wq, wk, wv, ctx_in, mask, q_cos, q_sin, k_cos, k_sin, q_dram):
    ident, w, stage = shared.ident, shared.w, shared.stage
    w_hi, w_lo, q_stored = shared.w_hi, shared.w_lo, shared.q_stored

    def sb(name, shape, dt=F32):
        return ctx.enter_context(nc.sbuf_tensor(name, shape, dt))

    def sem(name):
        return ctx.enter_context(nc.semaphore(name))

    x_tok = sb("q_x_tok", [ROWS, NTT, D])
    stats = sb("q_stats", [ROWS, NTT, 6])
    mv = sb("q_mv", [ROWS, NTT, 2])
    var = sb("q_var", [ROWS, NTT])
    std = sb("q_std", [ROWS, NTT])
    rstd = sb("q_rstd", [ROWS, NTT])
    xn = sb("q_xn", [ROWS, NTT, D])
    xT = [sb(f"xT_{n}", [P, DC, TOK], F32R) for n in ("hi", "lo")]
    wq_raw = sb("wq_raw", [P, 2, DC, GW])
    wq_s = [sb(f"wq_{n}", [P, 2, DC, GW], F32R) for n in ("hi", "lo")]
    cos_t = sb("q_cos_t", [P, SQ])
    sin_t = sb("q_sin_t", [P, SQ])
    q_swap = sb("q_swap", [P, 2, B, SQ])
    q_part = sb("q_part", [P, 2, B, SQ])
    q_rot = [sb("q_rot", [P, B, REP, SQ]), shared.head_rows]
    xT_banks = ctx.enter_context(nc.psum_tensor("xT_banks", [P, DC, BANK], F32))
    q_banks = ctx.enter_context(nc.psum_tensor("q_banks", [P, REP, BANK], F32))

    sp_passed = sem("q_sp_passed")
    x_loaded, tables_loaded = [sem(f"x_loaded{t}") for t in range(NTT)], sem("q_tables_loaded")
    wq_loaded = [sem(f"wq_loaded{i}") for i in range(2)]
    wq_first = [sem(f"wq_first{h}") for h in range(REP)]
    first_hi, first_lo = sem("wq_first_hi_ready"), sem("wq_first_lo_ready")
    cleared, ident_ready = sem("ident_cleared"), sem("ident_ready")
    stats_ready, mv_ready, var_ready, std_ready, rstd_ready, xn_ready = (
        sem(f"q_{n}_ready") for n in ("stats", "mv", "var", "std", "rstd", "xn"))
    xT_banked, xT_hi, xT_lo = sem("xT_banked"), sem("xT_hi_ready"), sem("xT_lo_ready")
    wq_hi, wq_lo = sem("wq_hi_ready"), sem("wq_lo_ready")
    q_ready, q_free, q_swapped, q_sined, q_rotated = (
        sem(n) for n in ("q_ready", "q_free", "q_swapped", "q_sined", "q_rotated"))
    swap_free = sem("q_swap_free")

    x_v = x.rearrange("(t b) s d -> (b s) t d", t=NTT)
    wq_v = wq.rearrange("(c p) n -> p c n", p=P)
    w_v = [m.rearrange("(c p) n -> c p n", p=P) for m in (wk, wv)]
    pairs = HKV // 2
    heads2 = 2 * REP

    block = ctx.enter_context(nc.Block())

    @block.sync
    def _(sp):
        for u in range(2):
            sp.sem_inc(q_stored[u], 16)
        for counted in (wq_hi, wq_lo):
            sp.sem_inc(counted, 1)
        sp.sem_inc(wq_loaded[0], 16)
        for t in range(NTT):
            sp.dma_start(x_tok[:, t, :], x_v[:, t]).then_inc(x_loaded[t], 16)
        for h in range(REP):
            head = slice(h * DH, (h + 1) * DH)
            sp.dma_start(wq_raw[:, 0, :, head], wq_v[:, :, head]).then_inc(wq_first[h], 16)
        sp.dma_start(cos_t[:, :], q_cos).then_inc(tables_loaded, 16)
        sp.dma_start(sin_t[:, :], q_sin).then_inc(tables_loaded, 16)
        sp.dma_start(wq_raw[:, 1], wq_v[:, :, GW:2 * GW]).then_inc(wq_loaded[1], 16)
        for n in range(2):
            sp.dma_start(stage[:, n, 0:HKV * DH], w_v[n][0]).then_inc(shared.stage_loaded[n], 16)

        def two_groups(i, last):
            for u in range(2):
                if not last:
                    sp.wait_ge(wq_hi, i * 2 + (u + 1))
                    wait_apart(sp, wq_lo, i * 2 + (u + 1), sp_passed)
                    src = wq_v[:, :, bass.ds(i * (2 * GW) + (2 + u) * GW, GW)]
                    sp.dma_start(wq_raw[:, u], src).then_inc(wq_loaded[u], 16)
                wait_apart(sp, w_lo, i * 2 + (u + 1), sp_passed)
                if not last:
                    sp.dma_start(stage[:, u, 0:HKV * DH],
                                 w_v[u][bass.ds(i + 1, 1)].rearrange("c p n -> p (c n)")).then_inc(shared.stage_loaded[u], 16)
                else:
                    load_context(nc, sp, shared, context_views(ctx_in), 0, u)
                wait_apart(sp, q_rotated, i * heads2 + (u + 1) * REP, sp_passed)
                dst = q_dram[bass.ds(i * 2 + u, 1)].rearrange("g p b n -> p (g b n)")
                sp.dma_start(dst, q_rot[u][:, :, :, :].rearrange("p b h s -> p (b h s)")).then_inc(q_stored[u], 16)

        sp.wait_ge(first_lo, REP)
        with sp.Fori(0, pairs - 1) as i:
            two_groups(i, False)
        for n, table in enumerate((k_cos, k_sin)):
            sp.dma_start(shared.tables[:, n], table).then_inc(shared.tables_loaded, 16)
        load_mask(sp, shared, mask, 0)
        two_groups(pairs - 1, True)
        sp.wait_ge(q_stored[0], 16 * (pairs + 1))

    @block.gpsimd
    def _(pool):
        nc.gpsimd.memset(ident[:, :], 0.0).then_inc(cleared, 1)
        pool.wait_ge(cleared, 1)
        nc.gpsimd.affine_select(out=ident[:, :], in_=ident[:, :], compare_op=ALU.not_equal, fill=1.0,
                                base=0, pattern=[[-1, P]], channel_multiplier=1).then_inc(ident_ready, 1)

        def wq_low(n, u):
            pool.wait_ge(wq_hi, n + 1)
            nc.gpsimd.tensor_tensor(wq_s[1][:, u], wq_raw[:, u], f32(wq_s[0][:, u]), ALU.subtract).then_inc(wq_lo, 1)

        def two_groups(i, last):
            for u in range(2):
                if not (last and u == 1):
                    wq_low(i * 2 + (u + 1), 1 - u)
                pool.wait_ge(w_hi, i * 2 + (u + 1))
                nc.gpsimd.tensor_tensor(w[u][1][:, bass.ds(i, 1), :], stage[:, u:u + 1, 0:HKV * DH],
                                        f32(w[u][0][:, bass.ds(i, 1), :]), ALU.subtract).then_inc(w_lo, 1)

        for h in range(REP):
            head = slice(h * DH, (h + 1) * DH)
            pool.wait_ge(first_hi, h + 1)
            nc.gpsimd.tensor_tensor(wq_s[1][:, 0, :, head], wq_raw[:, 0, :, head], f32(wq_s[0][:, 0, :, head]),
                                    ALU.subtract).then_inc(first_lo, 1)
        with pool.Fori(0, pairs - 1) as i:
            two_groups(i, False)
        two_groups(pairs - 1, True)

    @block.scalar
    def _(act):
        act.wait_ge(var_ready, 1)
        nc.scalar.activation(std[:, :], var[:, :], ACT.Sqrt).then_inc(std_ready, 1)

        def split_wq(n, u):
            act.wait_ge(wq_loaded[u], (n - u) * 8 + 16)
            nc.scalar.activation(wq_s[0][:, u], wq_raw[:, u], ACT.Copy).then_inc(wq_hi, 1)

        for c in range(DC):
            head = slice(c * DH, (c + 1) * DH)
            act.wait_ge(wq_first[c], 16)
            nc.scalar.activation(wq_s[0][:, 0, :, head], wq_raw[:, 0, :, head], ACT.Copy).then_inc(first_hi, 1)
            act.wait_ge(xT_banked, c + 1)
            nc.scalar.activation(xT[0][:, c, :], xT_banks[:, c, 0:TOK], ACT.Copy).then_inc(xT_hi, 1)

        def two_groups(i, last):
            for u in range(2):
                if not (last and u == 1):
                    split_wq(i * 2 + (u + 1), 1 - u)
                for hh in range(REP):
                    act.wait_ge(q_ready, i * heads2 + (u * REP + hh + 1))
                    act.wait_ge(swap_free, i * heads2 + (u * REP + hh + 1))
                    for lo in range(2):
                        nc.scalar.activation(
                            q_swap[lo * HALF:(lo + 1) * HALF, hh % 2].rearrange("p b s -> p (b s)"),
                            q_banks[(1 - lo) * HALF:(2 - lo) * HALF, hh, 0:TOK], ACT.Copy).then_inc(q_swapped, 1)
                    if hh == (0 if last and u == 1 else 2):
                        act.wait_ge(shared.stage_loaded[u], i * 16 + 16)
                        nc.scalar.activation(w[u][0][:, bass.ds(i, 1), :], stage[:, u:u + 1, 0:HKV * DH],
                                             ACT.Copy).then_inc(w_hi, 1)

        with act.Fori(0, pairs - 1) as i:
            two_groups(i, False)
        two_groups(pairs - 1, True)

    @block.tensor
    def _(pe):
        pe.wait_ge(ident_ready, 1)
        for c in range(DC):
            for t in range(NTT):
                if c == 0:
                    pe.wait_ge(xn_ready, t + 1)
                mm = nc.tensor.transpose(xT_banks[:, c, t * ROWS:(t + 1) * ROWS], xn[:, t, c * P:(c + 1) * P],
                                         ident[0:ROWS, 0:ROWS])
            mm.then_inc(xT_banked, 1)

        def two_groups(i):
            for u in range(2):
                pe.wait_ge(wq_lo, i * 2 + (u + 1))
                for hh in range(REP):
                    pe.wait_ge(q_free, i * heads2 + (u * REP + hh + 1))
                    if u == 0:
                        pe.wait_ge(first_lo, hh + 1)
                    for c in range(DC):
                        if u == 0 and hh == 0:
                            pe.wait_ge(xT_lo, c + 1)
                        for n, (a, m) in enumerate(PASSES):
                            mm = nc.tensor.matmul(q_banks[:, hh, 0:TOK], wq_s[a][:, u, c, hh * DH:(hh + 1) * DH],
                                                  xT[m][:, c, :], start=(c == 0 and n == 0),
                                                  stop=(c == DC - 1 and n == len(PASSES) - 1))
                    mm.then_inc(q_ready, 1)

        with pe.Fori(0, pairs) as i:
            two_groups(i)

    @block.vector
    def _(dve):
        dve.sem_inc(q_free, REP)
        dve.sem_inc(swap_free, 2)
        for t in range(NTT):
            dve.wait_ge(x_loaded[t], 16)
            nc.vector.bn_stats(stats[:, t], x_tok[:, t]).then_inc(stats_ready, 1)
        for t in range(NTT):
            dve.wait_ge(stats_ready, t + 1)
            nc.vector.bn_aggr(mv[:, t], stats[:, t]).then_inc(mv_ready, 1)
        dve.wait_ge(mv_ready, NTT)
        nc.vector.tensor_scalar(var[:, :], mv[:, :, 1], EPS, None, ALU.add).then_inc(var_ready, 1)
        dve.wait_ge(std_ready, 1)
        nc.vector.reciprocal(rstd[:, :], std[:, :]).then_inc(rstd_ready, 1)
        dve.wait_ge(rstd_ready, 1)
        for t in range(NTT):
            nc.vector.tensor_scalar(xn[:, t], x_tok[:, t], mv[:, t, 0:1], rstd[:, t:t + 1],
                                    ALU.subtract, ALU.mult).then_inc(xn_ready, 1)

        for c in range(DC):
            dve.wait_ge(xT_hi, c + 1)
            nc.vector.tensor_tensor(xT[1][:, c, :], xT_banks[:, c, 0:TOK], f32(xT[0][:, c, :]),
                                    ALU.subtract).then_inc(xT_lo, 1)
        dve.wait_ge(tables_loaded, 32)
        cos_b = cos_t[:, None, :].broadcast_to([P, B, SQ])
        sin_b = sin_t[:, None, :].broadcast_to([P, B, SQ])

        def two_groups(i):
            for u in range(2):
                dve.wait_ge(q_stored[u], i * 16 + 16)
                for hh in range(REP):
                    n = u * REP + hh
                    s = hh % 2
                    dve.wait_ge(q_swapped, i * (2 * heads2) + 2 * (n + 1))
                    nc.vector.tensor_tensor(q_part[:, s], q_banks[:, hh, 0:TOK].rearrange("p (b s) -> p b s", b=B),
                                            cos_b, ALU.mult).then_inc(q_free, 1)
                    nc.vector.tensor_tensor(q_swap[:, s], q_swap[:, s], sin_b, ALU.mult).then_inc(q_sined, 1)
                    dve.wait_ge(q_free, i * heads2 + (REP + n + 1))
                    dve.wait_ge(q_sined, i * heads2 + (n + 1))
                    nc.vector.tensor_tensor(q_rot[u][:, :, hh, :], q_part[:, s], q_swap[:, s],
                                            ALU.add).then_inc(q_rotated, 1)
                    dve.wait_ge(q_rotated, i * heads2 + (n + 1))
                    dve.sem_inc(swap_free, 1)

        with dve.Fori(0, pairs) as i:
            two_groups(i)


def attention_part(nc, ctx, shared, cT, ctx_in, mask, wo, q_dram, inv_dram, attn_dram):
    ident, stage, w, tables, mask_t = shared.ident, shared.stage, shared.w, shared.tables, shared.mask_t
    stage_loaded, attn, attn_stored = shared.stage_loaded, shared.attn, shared.attn_stored

    def sb(name, shape, dt=F32):
        return ctx.enter_context(nc.sbuf_tensor(name, shape, dt))

    def ps(name, n):
        return ctx.enter_context(nc.psum_tensor(name, [P, n, BANK], F32))

    def sem(name):
        return ctx.enter_context(nc.semaphore(name))

    def halves(name, shape):
        return [sb(f"{name}_{h}", shape, F32R) for h in ("hi", "lo")]

    v = halves("v", [ST, NT, PAIR])
    k = halves("k", [P, SK])
    k_swap, k_rot = (shared.k_work[:, n * 2 * SC:(n + 1) * 2 * SC].rearrange("p (s n) -> p s n", s=2) for n in range(2))
    prob = [sb(f"prob{h}", [ROWS, SK]) for h in range(HALVES)]
    pT = sb("pT", [ST, PT_SLOTS, 2, 2, GQ], F32R)
    q_raw = sb("q_raw", [P, 2, GQ])
    q = halves("q", [P, GQ])
    chunk_max = sb("chunk_max", [ROWS, HALVES, NC])
    neg_max = sb("neg_max", [ROWS, HALVES])
    row_sum = sb("row_sum", [ROWS, HALVES])
    inv_sum = sb("inv_sum", [ROWS, HALVES])
    inv_b = sb("inv_b", [P, GQ])
    o_lo = sb("o_lo", [P, GQ])
    o_sum = sb("o_sum", [P, GQ])
    k_banks, sv_banks, t_banks, o_banks = ps("k_banks", RING), ps("sv_banks", RING), ps("t_banks", RING), ps("o_banks", RING)

    q_loaded = [sem(f"q_loaded{i}") for i in range(2)]
    sp_passed, dve_passed = sem("sp_passed"), sem("dve_passed")
    sv_ready, sv_free, v_hi = sem("sv_ready"), sem("sv_free"), sem("v_hi_ready")
    k_ready, k_swapped, k_free, k_sined, k_rotated, k_hi, k_lo = (
        sem(n) for n in ("k_ready", "k_swapped", "k_free", "k_sined", "k_rotated", "k_hi_ready", "k_lo_ready"))
    t_ready, t_hi, t_free = sem("t_ready"), sem("t_hi_ready"), sem("t_free")
    o_ready, o_lo_copied, o_free, attn_ready = sem("o_ready"), sem("o_lo_copied"), sem("o_free"), sem("attn_ready")
    inv_stored, inv_loaded = sem("inv_stored"), sem("inv_loaded")
    max_ready, p_ready, inv_ready = sem("max_ready"), sem("p_ready"), sem("inv_ready")
    q_hi, q_lo = sem("q_hi_ready"), sem("q_lo_ready")

    w_loads = DC
    c_loads = STAGES // 2
    ctx_v = context_views(ctx_in)
    steps2 = HKV // 2

    def c_stage_ready(eng, b, m):
        n = m // STAGE
        eng.wait_ge(stage_loaded[n % 2], b * (16 * c_loads) + 16 * (w_loads + n // 2 + 1))

    def c_tile(m):
        return stage[0:ST, (m // STAGE) % 2, (m % STAGE) * D:(m % STAGE + 1) * D]

    block = ctx.enter_context(nc.Block())

    @block.sync
    def _(sp):
        def load_q(b, g):
            sp.dma_start(q_raw[:, g % 2], q_dram[g, :, bass.ds(b, 1)].rearrange("p b n -> p (b n)")).then_inc(q_loaded[g % 2], 16)

        for s in range(2):
            sp.sem_inc(attn_stored[s], 16)
        load_q(0, 0)
        sp.wait_ge(shared.q_stored[1], 16 * (HKV // 2 + 1))
        load_q(0, 1)
        for n in range(2, STAGES):
            sp.wait_ge(t_ready, (n - 1) * STAGE)
            load_context(nc, sp, shared, ctx_v, 0, n)

        def batch(b, last):
            if not last:
                for n in range(2):
                    wait_apart(sp, t_ready, t_item(b, 0, 0, last) + 1, sp_passed)
                    load_context(nc, sp, shared, ctx_v, b + 1, n)
            for g in range(HKV):
                if g == HKV - 1 and not last:
                    for n in range(2, STAGES):
                        wait_apart(sp, t_ready, c_item(b, (n - 1) * STAGE - 1) + 1, sp_passed)
                        load_context(nc, sp, shared, ctx_v, b + 1, n)
                    wait_apart(sp, sv_free, RING + sv_item(b, g, SCORES), sp_passed)
                    load_mask(sp, shared, mask, b + 1)
                if g == HKV - 1 and last:
                    sp.wait_ge(k_lo, k_item(b, g, NC - 1) + 1)
                    sp.wait_ge(sv_ready, sv_item(b, g - 1, SCORES + v_fill(g - 1, VT - 1)) + 1)
                    for u in range(2):
                        sp.wait_ge(attn_stored[u], 16 * (b * steps2 + 2))
                        load_attn(sp, shared, attn_dram, u, u)
                        if u == 0:
                            load_wo(sp, shared, wo, 1, 1)
                wait_apart(sp, inv_ready, b * (HKV * HALVES) + (g + 1) * HALVES, sp_passed)
                with nc.allow_non_contiguous_dma("224 numbers"):
                    sp.dma_start(inv_dram[g].rearrange("h r -> r h"), inv_sum[:, :]).then_inc(inv_stored, 16)
                wait_apart(sp, inv_stored, b * (16 * HKV) + 16 * (g + 1), sp_passed)
                sp.dma_start(inv_b[:, :], inv_dram[g:g + 1].rearrange("g h r -> g (h r)").broadcast_to([P, GQ])).then_inc(inv_loaded, 16)
                if g + 2 < HKV or not last:
                    wait_apart(sp, q_lo, b * HKV + (g + 1), sp_passed)
                    load_q(b + (g + 2) // HKV, (g + 2) % HKV)
                if g == 1 and last:
                    load_wo(sp, shared, wo, 0, 0)
                wait_apart(sp, attn_ready, b * HKV + (g + 1), sp_passed)
                sp.dma_start(attn_dram[g, :, bass.ds(b, 1)].rearrange("p b n -> p (b n)"), attn[:, g % 2]).then_inc(attn_stored[g % 2], 16)

        with sp.Fori(0, B - 1) as b:
            batch(b, False)
        batch(B - 1, True)

    @block.gpsimd
    def _(pool):
        def k_low(item, s, c):
            pool.wait_ge(k_hi, item + 1)
            nc.gpsimd.tensor_tensor(k[1][:, c * SC:(c + 1) * SC], k_rot[:, s], f32(k[0][:, c * SC:(c + 1) * SC]),
                                    ALU.subtract).then_inc(k_lo, 1)

        for c in range(NC):
            k_low(k_item(0, 0, c), c % 2, c)

        def batch(b, last):
            for g in range(1, HKV + 1 - last):
                for c in range(NC):
                    k_low(k_item(b, g, c), (g * NC + c) % 2, c)

        with pool.Fori(0, B - 1) as b:
            batch(b, False)
        batch(B - 1, True)
        wo_low(nc, pool, nc.gpsimd, shared, 0, 0)
        attn_low(nc, pool, nc.gpsimd, shared, 0, 0)

    @block.scalar
    def _(act):
        def k_exchange(item, s):
            act.wait_ge(k_ready, item + 1)
            if not isinstance(item, int) or item >= 2:
                act.wait_ge(k_rotated, item - 1)
            for lo in range(2):
                nc.scalar.activation(k_swap[lo * HALF:(lo + 1) * HALF, s],
                                     k_banks[(1 - lo) * HALF:(2 - lo) * HALF, s, 0:SC], ACT.Copy).then_inc(k_swapped, 1)

        def k_high(item, s, c):
            act.wait_ge(k_rotated, item + 1)
            nc.scalar.activation(k[0][:, c * SC:(c + 1) * SC], k_rot[:, s], ACT.Copy).then_inc(k_hi, 1)

        def c_high(item, s, m):
            act.wait_ge(t_ready, item + 1)
            nc.scalar.activation(cT[0][:, :, m * ST:(m + 1) * ST],
                                 t_banks[:, s, 0:DC * ST].rearrange("p (c s) -> p c s", c=DC), ACT.Copy).then_inc(t_hi, 1)

        def q_high(b, g):
            n = g % 2
            act.wait_ge(q_loaded[n], b * (16 * steps2) + 16 * (g // 2 + 1))
            nc.scalar.activation(q[0][:, :], q_raw[:, n], ACT.Copy).then_inc(q_hi, 1)

        def v_high(item, m):
            act.wait_ge(sv_ready, item + 1)
            nc.scalar.activation(v[0][:, 2 * m:2 * m + 2, :],
                                 sv_banks[0:ST, m % 2, :].rearrange("p (t n) -> p t n", t=2), ACT.Copy).then_inc(v_hi, 1)

        for what, (n, *_) in tasks(ACT_STEP["first"]):
            if what == "Q":
                q_high(0, 0)
            if what == "C":
                c_high(n, n % 2, n)
            if what == "swap":
                k_exchange(n, n % 2)
            if what == "K":
                k_high(n, n % 2, n)
            if what == "V":
                v_high(n, n)

        def step(b, g, last):
            kn = k_item(b, g + 1)
            kind = step_kind(g, last)
            for what, (n, *_) in tasks(ACT_STEP[kind]):
                s = ((g + 1) * NC + n) % 2
                if what in ("C", "T"):
                    t_bank = t_place(kind, what, n) % 2
                if what == "exp":
                    act.wait_ge(max_ready, b * (HKV * HALVES) + (g * HALVES + n + 1))
                    nc.scalar.activation(prob[n][:, :], prob[n][:, :], ACT.Exp, bias=neg_max[:, n:n + 1],
                                         accum_out=row_sum[:, n:n + 1]).then_inc(p_ready, 1)
                if what == "Q":
                    q_high(b, g + 1)
                if what == "swap":
                    k_exchange(kn + n, s)
                if what == "K":
                    k_high(kn + n, s, n)
                if what == "out":
                    act.wait_ge(o_ready, b * HKV + (g + 1))
                    nc.scalar.activation(o_lo[:, :], o_banks[:, g % 2, GQ:2 * GQ], ACT.Copy).then_inc(o_lo_copied, 1)
                if what == "wo":
                    wo_high(nc, act, shared, n, n)
                if what == "attn":
                    attn_high(nc, act, shared, n, n)
                if what == "V":
                    v_high(sv_item(b, g, SCORES + v_fill(g, n)), n)
                if what == "C":
                    c_high(c_item(b, n), t_bank, n)
                if what == "T":
                    act.wait_ge(t_ready, t_item(b, g, n, last) + 1)
                    nc.scalar.activation(pT[:, n % PT_SLOTS, :, 0, :],
                                         t_banks[0:ST, t_bank, 0:2 * GQ].rearrange("p (t n) -> p t n", t=2),
                                         ACT.Copy).then_inc(t_hi, 1)

        with act.Fori(0, B - 1) as b:
            for g in range(HKV):
                step(b, g, False)
        for g in range(HKV):
            step(B - 1, g, True)

    @block.tensor
    def _(pe):
        def k_part(item, s, g, c, d, context_item):
            if d == 0:
                pe.wait_ge(k_free, item + 1)
                if context_item is not None:
                    pe.wait_ge(t_free, context_item + (RING + 1))
            for n, (a, m) in enumerate(PASSES):
                mm = nc.tensor.matmul(k_banks[:, s, 0:SC], w[0][a][:, d, g * DH:(g + 1) * DH],
                                      cT[m][:, d, c * SC:(c + 1) * SC], start=(d == 0 and n == 0),
                                      stop=(d == DC - 1 and n == len(PASSES) - 1))
            if d == DC - 1:
                mm.then_inc(k_ready, 1)

        def v_part(item, g, m, t, context_item):
            if t == 0:
                pe.wait_ge(sv_free, item + 1)
            if context_item is not None:
                pe.wait_ge(t_free, context_item + (RING + 1))
            tile = 2 * m + t
            for d in range(DC):
                for n, (a, mv) in enumerate(PASSES):
                    mm = nc.tensor.matmul(sv_banks[0:ST, m % 2, t * PAIR:(t + 1) * PAIR],
                                          cT[a][:, d, tile * ST:(tile + 1) * ST], w[1][mv][:, d, g * DH:g * DH + PAIR],
                                          start=(d == 0 and n == 0), stop=(d == DC - 1 and n == len(PASSES) - 1))
            if t == 1:
                mm.then_inc(sv_ready, 1)

        def c_transposes(b, item, s, m):
            pe.wait_ge(t_free, item + 1)
            if m % STAGE == 0:
                c_stage_ready(pe, b, m)
            for d in range(DC):
                mm = nc.tensor.transpose(t_banks[:, s, d * ST:(d + 1) * ST], c_tile(m)[:, d * P:(d + 1) * P],
                                         ident[0:ST, 0:ST])
            mm.then_inc(t_ready, 1)

        def scores(b, g, i):
            h, c = divmod(i, NC)
            if i == 0:
                pe.wait_ge(q_lo, b * HKV + (g + 1))
            pe.wait_ge(sv_free, sv_item(b, g, i) + 1)
            if h == 0:
                pe.wait_ge(k_lo, k_item(b, g, c) + 1)
            for n, (a, m) in enumerate(PASSES):
                mm = nc.tensor.matmul(sv_banks[0:ROWS, i % 2, 0:SC], q[a][:, h * ROWS:(h + 1) * ROWS],
                                      k[m][:, c * SC:(c + 1) * SC], start=(n == 0), stop=(n == len(PASSES) - 1))
            mm.then_inc(sv_ready, 1)

        def transposes(b, g, s, j, last):
            pe.wait_ge(t_free, t_item(b, g, j, last) + 1)
            if j == 0:
                pe.wait_ge(p_ready, b * (HKV * HALVES) + (g + 1) * HALVES)
            for t in range(2):
                for h in range(HALVES):
                    col = t * GQ + h * ROWS
                    mm = nc.tensor.transpose(t_banks[0:ST, s, col:col + ROWS],
                                             prob[h][:, (2 * j + t) * ST:(2 * j + t + 1) * ST], ident[0:ROWS, 0:ROWS])
            mm.then_inc(t_ready, 1)

        def weigh(b, g, j, last):
            if j == 0:
                pe.wait_ge(o_free, b * HKV + (g + 1))
            pe.wait_ge(t_free, t_item(b, g, j, last) + (RING + 1))
            if g % 2 == 0 and j >= V_AHEAD:
                pe.wait_ge(sv_free, sv_item(b, g, SCORES + v_fill(g, j)) + (RING + 1))
            for t in range(2):
                first, final = j == 0 and t == 0, j == PT - 1 and t == 1
                for a in ((1, 0) if final else (0, 1)):
                    probs = pT[:, j % PT_SLOTS, t].rearrange("p h n -> p (h n)")[:, 0:(2 - a) * GQ]
                    mm = nc.tensor.matmul(o_banks[:, g % 2, 0:(2 - a) * GQ],
                                          v[a][:, 2 * j + t, (g % 2) * DH:(g % 2 + 1) * DH], probs,
                                          start=(first and a == 0), stop=(final and a == 0), skip_group_check=True)
            if j == PT - 1:
                mm.then_inc(o_ready, 1)

        for what, n in tasks(PE_STEP["first"]):
            if what == "C":
                c_transposes(0, n[0], n[0] % 2, *n)
            if what == "K":
                k_part(n[0], n[0] % 2, 0, *n, (n[0] + 1) * CT - 1)
            if what == "V":
                v_part(n[0], 0, *n, 2 * n[0] + n[1])

        def step(b, g, last):
            kind = step_kind(g, last)
            turn = kind == "turn"
            for what, n in tasks(PE_STEP[kind]):
                if what in ("C", "T"):
                    t_bank = t_place(kind, what, *n) % 2
                if what == "S":
                    scores(b, g, *n)
                if what == "K":
                    k_part(k_item(b, g + 1, n[0]), ((g + 1) * NC + n[0]) % 2, (g + 1) % HKV, *n,
                           c_item(b, (n[0] + 1) * CT - 1) if turn else None)
                if what == "V":
                    v_part(sv_item(b, g, SCORES + v_fill(g, n[0])), (g + g % 2) % HKV, *n,
                           c_item(b, 2 * n[0] + n[1]) if turn else None)
                if what == "C":
                    c_transposes(b + 1, c_item(b, *n), t_bank, *n)
                if what == "T":
                    transposes(b, g, t_bank, *n, last)
                if what == "PV":
                    weigh(b, g, *n, last)

        with pe.Fori(0, B - 1) as b:
            for g in range(HKV):
                step(b, g, False)
        for g in range(HKV):
            step(B - 1, g, True)

    @block.vector
    def _(dve):
        for ring in (k_free, sv_free, t_free, o_free):
            dve.sem_inc(ring, RING)

        def k_cos_part(item, s, c):
            dve.wait_ge(k_swapped, item * 2 + 2)
            if not isinstance(item, int) or item >= 2:
                dve.wait_ge(k_lo, item - 1)
            nc.vector.tensor_tensor(k_rot[:, s], k_banks[:, s, 0:SC], tables[:, 0, c * SC:(c + 1) * SC],
                                    ALU.mult).then_inc(k_free, 1)

        def k_sin_part(s, c):
            nc.vector.tensor_tensor(k_swap[:, s], k_swap[:, s], tables[:, 1, c * SC:(c + 1) * SC],
                                    ALU.mult).then_inc(k_sined, 1)

        def k_rotate(item, s):
            dve.wait_ge(k_free, item + (RING + 1))
            dve.wait_ge(k_sined, item + 1)
            nc.vector.tensor_tensor(k_rot[:, s], k_rot[:, s], k_swap[:, s], ALU.add).then_inc(k_rotated, 1)

        def c_low(item, s, m):
            dve.wait_ge(t_hi, item + 1)
            dst = slice(m * ST, (m + 1) * ST)
            nc.vector.tensor_tensor(cT[1][:, :, dst], t_banks[:, s, 0:DC * ST].rearrange("p (c s) -> p c s", c=DC),
                                    f32(cT[0][:, :, dst]), ALU.subtract).then_inc(t_free, 1)

        def q_low(b, g):
            dve.wait_ge(q_hi, b * HKV + (g + 1))
            nc.vector.tensor_tensor(q[1][:, :], q_raw[:, g % 2], f32(q[0][:, :]), ALU.subtract).then_inc(q_lo, 1)

        def v_low(item, m):
            dve.wait_ge(v_hi, item + 1)
            nc.vector.tensor_tensor(v[1][:, 2 * m:2 * m + 2, :], sv_banks[0:ST, m % 2, :].rearrange("p (t n) -> p t n", t=2),
                                    f32(v[0][:, 2 * m:2 * m + 2, :]), ALU.subtract).then_inc(sv_free, 1)

        dve.wait_ge(shared.tables_loaded, 32)
        for what, (n, *_) in tasks(DVE_STEP["first"]):
            if what == "Q":
                q_low(0, 0)
            if what == "C":
                c_low(n, n % 2, n)
            if what == "cos":
                k_cos_part(n, n % 2, n)
            if what == "sin":
                k_sin_part(n % 2, n)
            if what == "rot":
                k_rotate(n, n % 2)
            if what == "V":
                v_low(n, n)

        def step(b, g, last):
            kn = k_item(b, g + 1)
            if g == 0:
                dve.wait_ge(shared.mask_loaded, b * 32 + 32)
            kind = step_kind(g, last)
            for what, (n, *_) in tasks(DVE_STEP[kind]):
                s = ((g + 1) * NC + n) % 2
                if what in ("C", "T"):
                    t_bank = t_place(kind, what, n) % 2
                if what == "mask":
                    h, c = divmod(n, NC)
                    wait_apart(dve, sv_ready, sv_item(b, g, n) + 1, dve_passed)
                    nc.vector.tensor_tensor_reduce(prob[h][:, c * SC:(c + 1) * SC], sv_banks[0:ROWS, n % 2, 0:SC],
                                                   mask_t[:, c * SC:(c + 1) * SC], 1.0, LOWEST, ALU.add, ALU.max,
                                                   chunk_max[:, h, c:c + 1]).then_inc(sv_free, 1)
                if what == "max":
                    dve.wait_ge(sv_free, sv_item(b, g, (n + 1) * NC) + RING)
                    nc.vector.tensor_reduce(neg_max[:, n:n + 1], chunk_max[:, n, :], AX_X, ALU.max,
                                            negate=True).then_inc(max_ready, 1)
                if what == "inv":
                    for h in range(HALVES):
                        dve.wait_ge(p_ready, b * (HKV * HALVES) + (g * HALVES + h + 1))
                        nc.vector.reciprocal(inv_sum[:, h:h + 1], row_sum[:, h:h + 1]).then_inc(inv_ready, 1)
                if what == "Q":
                    q_low(b, g + 1)
                if what == "cos":
                    k_cos_part(kn + n, s, n)
                if what == "sin":
                    k_sin_part(s, n)
                if what == "rot":
                    k_rotate(kn + n, s)
                if what == "V":
                    v_low(b * (HKV // 2 * VT) + (V_AHEAD + g // 2 * VT + (g % 2) * V_REST + v_fill(g, n)), n)
                if what == "C":
                    c_low(c_item(b, n), t_bank, n)
                if what == "T":
                    dve.wait_ge(t_hi, t_item(b, g, n, last) + 1)
                    nc.vector.tensor_tensor(pT[:, n % PT_SLOTS, :, 1, :],
                                            t_banks[0:ST, t_bank, 0:2 * GQ].rearrange("p (t n) -> p t n", t=2),
                                            f32(pT[:, n % PT_SLOTS, :, 0, :]), ALU.subtract).then_inc(t_free, 1)
                if what == "out":
                    dve.wait_ge(o_lo_copied, b * HKV + (g + 1))
                    nc.vector.tensor_tensor(o_sum[:, :], o_banks[:, g % 2, 0:GQ], o_lo[:, :], ALU.add).then_inc(o_free, 1)
                    dve.wait_ge(o_free, b * HKV + (RING + g + 1))
                    dve.wait_ge(inv_loaded, b * (16 * HKV) + 16 * (g + 1))
                    dve.wait_ge(attn_stored[g % 2], b * (16 * steps2) + 16 * (g // 2 + 1))
                    nc.vector.tensor_tensor(attn[:, g % 2], o_sum[:, :], inv_b[:, :], ALU.mult).then_inc(attn_ready, 1)

        with dve.Fori(0, B - 1) as b:
            for g in range(HKV):
                step(b, g, False)
        for g in range(HKV):
            step(B - 1, g, True)


def attn_high(nc, act, shared, n, u):
    act.wait_ge(shared.attn_loaded[u], (n - u) * 8 + 16)
    nc.scalar.activation(shared.attn_s[0][:, u].rearrange("p h b s -> p b h s"), shared.attn_raw[u],
                         ACT.Copy).then_inc(shared.attn_hi, 1)


def wo_high(nc, act, shared, n, u):
    act.wait_ge(shared.wo_loaded[u], (n - u) * 8 + 16)
    nc.scalar.activation(shared.wo_s[0][:, u], shared.wo_raw[u], ACT.Copy).then_inc(shared.wo_hi, 1)


def attn_low(nc, eng, ops, shared, n, u):
    eng.wait_ge(shared.attn_hi, n + 1)
    ops.tensor_tensor(shared.attn_s[1][:, u].rearrange("p h b s -> p b h s"), shared.attn_raw[u],
                      f32(shared.attn_s[0][:, u]).rearrange("p h b s -> p b h s"), ALU.subtract).then_inc(shared.attn_lo, 1)


def wo_low(nc, eng, ops, shared, n, u):
    eng.wait_ge(shared.wo_hi, n + 1)
    ops.tensor_tensor(shared.wo_s[1][:, u], shared.wo_raw[u], f32(shared.wo_s[0][:, u]),
                      ALU.subtract).then_inc(shared.wo_lo, 1)


def output_part(nc, ctx, shared, x, wo, a_in, b_in, wr, g_xattn, g_ffn, attn_dram, out):
    def sb(name, shape, dt=F32):
        return ctx.enter_context(nc.sbuf_tensor(name, shape, dt))

    def sem(name):
        return ctx.enter_context(nc.semaphore(name))

    ident, attn_s, wo_s = shared.ident, shared.attn_s, shared.wo_s
    x_tok = sb("o_x_tok", [ROWS, NTT, D])
    y = sb("y", [ROWS, NTT, D])
    yn = sb("yn", [ROWS, NTT, D])
    res = sb("res", [ROWS, NTT, D])
    gate_raw = sb("gate_raw", [ROWS, 2])
    tanh_g = sb("tanh_g", [ROWS, 2])
    ar = sb("ar", [ER + EXPERTS, D])
    arT = sb("arT", [P, DC, ER + EXPERTS])
    b_raw = sb("b_raw", [P, DC, EXPERTS, RANK])
    bT = sb("bT", [ER, D])
    stats = sb("o_stats", [ROWS, NTT, 6])
    mv = sb("o_mv", [ROWS, NTT, 2])
    var = sb("o_var", [ROWS, NTT])
    std = sb("o_std", [ROWS, NTT])
    rstd = sb("o_rstd", [ROWS, NTT])
    yT = sb("yT", [P, NTT, DC, ROWS])
    z = sb("z", [ROWS, NTT, ER + EXPERTS])
    earlier = sb("earlier", [ROWS, NTT, EXPERTS, EXPERTS])
    beats = sb("beats", [ROWS, NTT, EXPERTS, EXPERTS])
    ties = sb("ties", [ROWS, NTT, EXPERTS, EXPERTS])
    rank = sb("rank", [ROWS, NTT, EXPERTS])
    top = sb("top", [ROWS, NTT])
    shifted = sb("shifted", [ROWS, NTT, EXPERTS])
    exps = sb("exps", [ROWS, NTT, EXPERTS])
    gates = sb("gates", [ROWS, NTT, EXPERTS])
    total = sb("total", [ROWS, NTT])
    inv_total = sb("inv_total", [ROWS, NTT])
    mid = sb("mid", [ROWS, NTT, EXPERTS, RANK])
    midT = sb("midT", [ER, TOK])
    acc = ctx.enter_context(nc.psum_tensor("acc", [P, NTT, BANK], F32))
    yT_banks = ctx.enter_context(nc.psum_tensor("yT_banks", [P, NTT, BANK], F32))

    sp_passed = sem("o_sp_passed")
    x_loaded, small_loaded = sem("o_x_loaded"), sem("small_loaded")
    group_done, acc_done, tanh_ready, y_ready = sem("group_done"), sem("acc_done"), sem("tanh_ready"), sem("y_ready")
    stats_ready, mv_ready, var_ready, std_ready, rstd_ready, yn_ready = (
        sem(f"o_{n}_ready") for n in ("stats", "mv", "var", "std", "rstd", "yn"))
    small_banked, small_copied = sem("small_banked"), sem("small_copied")
    yT_banked, yT_ready, z_banked, z_ready = sem("yT_banked"), sem("yT_ready"), sem("z_banked"), sem("z_ready")
    gate_steps, earlier_steps, exp_ready, mid_ready = sem("gate_steps"), sem("earlier_steps"), sem("exp_ready"), sem("mid_ready")
    midT_banked, midT_ready, delta_ready, res_ready, stored = (
        sem(n) for n in ("midT_banked", "midT_ready", "delta_ready", "res_ready", "stored"))

    x_v = x.rearrange("(t b) s d -> (b s) t d", t=NTT)
    out_v = out.rearrange("(t b) s d -> (b s) t d", t=NTT)
    pairs = HKV // 2
    SMALL = 16 * (4 + DC)

    block = ctx.enter_context(nc.Block())

    @block.sync
    def _(sp):
        def two_groups(i):
            for u in range(2):
                sp.wait_ge(shared.attn_lo, i * 2 + (u + 1))
                wait_apart(sp, shared.wo_lo, i * 2 + (u + 1), sp_passed)
                load_wo(sp, shared, wo, i * 2 + (2 + u), u)
                load_attn(sp, shared, attn_dram, i * 2 + (2 + u), u)

        for u in range(2):
            sp.wait_ge(shared.attn_stored[u], 16 * (B * (HKV // 2) + 1))
        two_groups(0)
        sp.dma_start(x_tok[:, :, :], x_v).then_inc(x_loaded, 16)
        with nc.allow_non_contiguous_dma("small operands"):
            sp.dma_start(ar[0:ER, :], a_in.rearrange("e r f -> (e r) f")).then_inc(small_loaded, 16)
            sp.dma_start(ar[ER:ER + EXPERTS, :], wr).then_inc(small_loaded, 16)
            for n, gate in enumerate((g_xattn, g_ffn)):
                sp.dma_start(gate_raw[:, n:n + 1], gate.rearrange("(a n) -> a n", a=1).broadcast_to([ROWS, 1])).then_inc(small_loaded, 16)
            for c in range(DC):
                sp.dma_start(b_raw[:, c], b_in[:, c * P:(c + 1) * P, :].rearrange("e o r -> o e r")).then_inc(small_loaded, 16)
        with sp.Fori(1, pairs - 1) as i:
            two_groups(i)
        for t in range(NTT):
            sp.wait_ge(res_ready, t + 1)
            sp.dma_start(out_v[:, t], res[:, t]).then_inc(stored, 16)
        sp.wait_ge(stored, 16 * NTT)

    @block.gpsimd
    def _(pool):
        nc.gpsimd.memset(earlier[:, :, :, :], 1.0).then_inc(earlier_steps, 1)
        pool.wait_ge(earlier_steps, 1)
        nc.gpsimd.affine_select(out=earlier[:, :, :, :], in_=earlier[:, :, :, :], compare_op=ALU.is_gt, fill=0.0, base=0,
                                pattern=[[0, NTT], [1, EXPERTS], [-1, EXPERTS]], channel_multiplier=0).then_inc(earlier_steps, 1)

    @block.scalar
    def _(act):
        def y_transposed(t):
            act.wait_ge(yT_banked, t + 1)
            nc.scalar.activation(yT[:, t], yT_banks[:, t, 0:DC * ROWS].rearrange("p (c n) -> p c n", c=DC),
                                 ACT.Copy).then_inc(yT_ready, 1)

        wo_high(nc, act, shared, 1, 1)
        attn_high(nc, act, shared, 1, 1)
        with act.Fori(1, pairs) as i:
            for u in range(2):
                act.wait_ge(group_done, i * 2 + (u - 1))
                wo_high(nc, act, shared, i * 2 + u, u)
                attn_high(nc, act, shared, i * 2 + u, u)
        act.wait_ge(small_loaded, SMALL)
        nc.scalar.activation(tanh_g[:, :], gate_raw[:, :], ACT.Tanh).then_inc(tanh_ready, 1)

        def y_std(t):
            act.wait_ge(var_ready, t + 1)
            nc.scalar.activation(std[:, t:t + 1], var[:, t:t + 1], ACT.Sqrt).then_inc(std_ready, 1)

        for t in range(NTT - 1):
            y_std(t)
        y_transposed(0)
        y_transposed(1)
        y_std(NTT - 1)
        y_transposed(2)
        y_transposed(3)
        act.wait_ge(gate_steps, 4)
        nc.scalar.activation(exps[:, :, :], shifted[:, :, :], ACT.Exp).then_inc(exp_ready, 1)

    @block.tensor
    def _(pe):
        def project(t, h, u, first, last):
            for n, (a, m) in enumerate(PASSES):
                mm = nc.tensor.matmul(acc[0:ROWS, t, :],
                                      attn_s[a][:, u, h].rearrange("p b s -> p (b s)")[:, t * ROWS:(t + 1) * ROWS],
                                      wo_s[m][:, u, h, :], start=(first and n == 0),
                                      stop=(last and n == len(PASSES) - 1), skip_group_check=True)
            return mm

        def group(g, u, first=False):
            pe.wait_ge(shared.attn_lo, g + 1)
            pe.wait_ge(shared.wo_lo, g + 1)
            for h in range(REP):
                for t in range(NTT):
                    mm = project(t, h, u, first and h == 0, False)
            mm.then_inc(group_done, 1)

        group(0, 0, True)
        group(1, 1)
        with pe.Fori(1, pairs - 1) as i:
            for u in range(2):
                group(i * 2 + u, u)
        pe.wait_ge(small_loaded, SMALL)
        n = ER + EXPERTS
        for c in range(DC):
            mm = nc.tensor.transpose(yT_banks[:, 0, c * n:(c + 1) * n], ar[:, c * P:(c + 1) * P], ident[0:n, 0:n])
        mm.then_inc(small_banked, 1)
        for c in range(DC):
            mm = nc.tensor.transpose(yT_banks[0:ER, 1, c * P:(c + 1) * P], b_raw[:, c].rearrange("p e r -> p (e r)"), ident[:, :])
        mm.then_inc(small_banked, 1)
        group(HKV - 2, 0)
        pe.wait_ge(shared.attn_lo, HKV)
        pe.wait_ge(shared.wo_lo, HKV)
        for t in range(NTT):
            for h in range(REP):
                mm = project(t, h, 1, False, h == REP - 1)
            mm.then_inc(acc_done, 1)

        pe.wait_ge(small_copied, 2)

        def transpose_y(t):
            pe.wait_ge(yn_ready, t + 1)
            for c in range(DC):
                mm = nc.tensor.transpose(yT_banks[:, t, c * ROWS:(c + 1) * ROWS], yn[:, t, c * P:(c + 1) * P], ident[0:ROWS, 0:ROWS])
            mm.then_inc(yT_banked, 1)

        def mid_and_logits(t):
            pe.wait_ge(yT_ready, t + 1)
            for c in range(DC):
                mm = nc.tensor.matmul(acc[0:ROWS, 0, t * n:(t + 1) * n], yT[:, t, c], arT[:, c, :],
                                      start=(c == 0), stop=(c == DC - 1))
            mm.then_inc(z_banked, 1)

        for t in range(NTT):
            transpose_y(t)
            if t > 0:
                mid_and_logits(t - 1)
        mid_and_logits(NTT - 1)
        pe.wait_ge(mid_ready, 1)
        for t in range(NTT):
            mm = nc.tensor.transpose(yT_banks[0:ER, 0, t * ROWS:(t + 1) * ROWS], mid[:, t].rearrange("p e r -> p (e r)"), ident[0:ROWS, 0:ROWS])
        mm.then_inc(midT_banked, 1)
        pe.wait_ge(midT_ready, 1)
        for t in range(NTT):
            nc.tensor.matmul(acc[0:ROWS, t, :], midT[:, t * ROWS:(t + 1) * ROWS], bT[:, :], start=True, stop=True).then_inc(delta_ready, 1)

    @block.vector
    def _(dve):
        def split_group(n, u):
            wo_low(nc, dve, nc.vector, shared, n, u)
            attn_low(nc, dve, nc.vector, shared, n, u)

        split_group(1, 1)
        with dve.Fori(1, pairs) as i:
            for u in range(2):
                split_group(i * 2 + u, u)
        dve.wait_ge(small_banked, 1)
        nc.vector.tensor_copy(arT[:, :, :], yT_banks[:, 0, 0:DC * (ER + EXPERTS)].rearrange("p (c n) -> p c n", c=DC)).then_inc(small_copied, 1)
        dve.wait_ge(small_banked, 2)
        nc.vector.tensor_copy(bT[:, :], yT_banks[0:ER, 1, :]).then_inc(small_copied, 1)
        dve.wait_ge(x_loaded, 16)
        dve.wait_ge(tanh_ready, 1)
        for t in range(NTT):
            dve.wait_ge(acc_done, t + 1)
            nc.vector.scalar_tensor_tensor(out=y[:, t], in0=acc[0:ROWS, t, :], scalar=tanh_g[:, 0:1], in1=x_tok[:, t],
                                           op0=ALU.mult, op1=ALU.add).then_inc(y_ready, 1)
            dve.wait_ge(y_ready, t + 1)
            nc.vector.bn_stats(stats[:, t], y[:, t]).then_inc(stats_ready, 1)
            dve.wait_ge(stats_ready, t + 1)
            nc.vector.bn_aggr(mv[:, t], stats[:, t]).then_inc(mv_ready, 1)
            dve.wait_ge(mv_ready, t + 1)
            nc.vector.tensor_scalar(var[:, t:t + 1], mv[:, t, 1:2], EPS, None, ALU.add).then_inc(var_ready, 1)
            dve.wait_ge(std_ready, t + 1)
            nc.vector.reciprocal(rstd[:, t:t + 1], std[:, t:t + 1]).then_inc(rstd_ready, 1)
            dve.wait_ge(rstd_ready, t + 1)
            nc.vector.tensor_scalar(yn[:, t], y[:, t], mv[:, t, 0:1], rstd[:, t:t + 1], ALU.subtract, ALU.mult).then_inc(yn_ready, 1)
        dve.wait_ge(z_banked, NTT)
        nc.vector.tensor_copy(z[:, :, :], acc[0:ROWS, 0, 0:NTT * (ER + EXPERTS)].rearrange("p (t n) -> p t n", t=NTT)).then_inc(z_ready, 1)
        dve.wait_ge(z_ready, 1)
        logits = z[:, :, ER:ER + EXPERTS]
        square = [ROWS, NTT, EXPERTS, EXPERTS]
        of_e = logits[:, :, :, None].broadcast_to(square)
        of_j = logits[:, :, None, :].broadcast_to(square)
        nc.vector.tensor_reduce(top[:, :], logits, AX_X, ALU.max).then_inc(gate_steps, 1)
        nc.vector.tensor_tensor(beats[:, :, :, :], of_j, of_e, ALU.is_gt).then_inc(gate_steps, 1)
        nc.vector.tensor_tensor(ties[:, :, :, :], of_j, of_e, ALU.is_equal).then_inc(gate_steps, 1)
        dve.wait_ge(gate_steps, 3)
        nc.vector.tensor_tensor(shifted[:, :, :], logits, top[:, :, None].broadcast_to([ROWS, NTT, EXPERTS]), ALU.subtract).then_inc(gate_steps, 1)
        dve.wait_ge(earlier_steps, 2)
        nc.vector.tensor_tensor(ties[:, :, :, :], ties[:, :, :, :], earlier[:, :, :, :], ALU.mult).then_inc(gate_steps, 1)
        dve.wait_ge(gate_steps, 5)
        nc.vector.tensor_tensor(beats[:, :, :, :], beats[:, :, :, :], ties[:, :, :, :], ALU.add).then_inc(gate_steps, 1)
        dve.wait_ge(gate_steps, 6)
        nc.vector.tensor_reduce(rank[:, :, :], beats[:, :, :, :], AX_X, ALU.add).then_inc(gate_steps, 1)
        dve.wait_ge(gate_steps, 7)
        dve.wait_ge(exp_ready, 1)
        nc.vector.scalar_tensor_tensor(out=gates[:, :, :], in0=rank[:, :, :], scalar=2.0, in1=exps[:, :, :],
                                       op0=ALU.is_lt, op1=ALU.mult).then_inc(gate_steps, 1)
        dve.wait_ge(gate_steps, 8)
        nc.vector.tensor_reduce(total[:, :], gates[:, :, :], AX_X, ALU.add).then_inc(gate_steps, 1)
        dve.wait_ge(gate_steps, 9)
        nc.vector.reciprocal(inv_total[:, :], total[:, :]).then_inc(gate_steps, 1)
        dve.wait_ge(gate_steps, 10)
        nc.vector.scalar_tensor_tensor(out=gates[:, :, :], in0=gates[:, :, :], scalar=LORA_SCALE,
                                       in1=inv_total[:, :, None].broadcast_to([ROWS, NTT, EXPERTS]),
                                       op0=ALU.mult, op1=ALU.mult).then_inc(gate_steps, 1)
        dve.wait_ge(gate_steps, 11)
        nc.vector.tensor_tensor(mid[:, :, :, :], z[:, :, 0:ER].rearrange("p t (e r) -> p t e r", e=EXPERTS),
                                gates[:, :, :, None].broadcast_to([ROWS, NTT, EXPERTS, RANK]), ALU.mult).then_inc(mid_ready, 1)
        dve.wait_ge(midT_banked, 1)
        nc.vector.tensor_copy(midT[:, :], yT_banks[0:ER, 0, 0:TOK]).then_inc(midT_ready, 1)
        for t in range(NTT):
            dve.wait_ge(delta_ready, t + 1)
            nc.vector.scalar_tensor_tensor(out=res[:, t], in0=acc[0:ROWS, t, :], scalar=tanh_g[:, 1:2], in1=y[:, t],
                                           op0=ALU.mult, op1=ALU.add).then_inc(res_ready, 1)


def flamingo_block(nc, x, ctx_in, mask, g_xattn, g_ffn, wq, wk, wv, wo, a_in, b_in, wr,
                   q_cos, q_sin, k_cos, k_sin, out):
    q_dram = nc.dram_tensor("q_by_head", (HKV, P, B, GQ), F32).ap()
    attn_dram = nc.dram_tensor("attn_by_head", (HKV, P, B, GQ), F32).ap()
    inv_dram = nc.dram_tensor("inv_by_head", (HKV, HALVES, ROWS), F32).ap()
    with ExitStack() as whole:
        shared = Shared(nc, whole)
        with ExitStack() as ctx:
            query_part(nc, ctx, shared, x, wq, wk, wv, ctx_in, mask, q_cos, q_sin, k_cos, k_sin, q_dram)
        cT = [whole.enter_context(nc.sbuf_tensor(f"cT_{h}", [P, DC, SK], F32R)) for h in ("hi", "lo")]
        shared.output_operands(cT)
        with ExitStack() as ctx:
            attention_part(nc, ctx, shared, cT, ctx_in, mask, wo, q_dram, inv_dram, attn_dram)
        with ExitStack() as ctx:
            output_part(nc, ctx, shared, x, wo, a_in, b_in, wr, g_xattn, g_ffn, attn_dram, out)


def rotary_tables(positions, scale):
    inv_freq = (1.0 / np.float32(10000.0) ** (np.arange(0, DH, 2, dtype=np.float32) / np.float32(DH))).astype(np.float32)
    ang = (inv_freq[:, None] * np.arange(positions, dtype=np.float32)[None, :]).astype(np.float32)
    cos, sin = np.cos(ang).astype(np.float32), np.sin(ang).astype(np.float32)
    return (np.concatenate([cos, cos]) * np.float32(scale)).astype(np.float32), \
        (np.concatenate([-sin, sin]) * np.float32(scale)).astype(np.float32)


_INS = ['x', 'ctx_4096', 'mask_BxSxS2_ff0', 'g_xattn', 'g_ffn', 'L0_xattn_wq', 'L0_xattn_wk', 'L0_xattn_wv',
        'L0_xattn_wo', 'L0_ffn_A', 'L0_ffn_B', 'L0_ffn_Wr']
_OUTS = [((B, SQ, D), 'float32')]


def kernel(**inputs):
    import numpy as _np
    import concourse.bacc as _bacc
    from concourse import mybir as _mybir
    from concourse.bass_utils import run_bass_kernel_spmd as _run

    nc = _bacc.Bacc("TRN2", target_bir_lowering=False, num_devices=1, dynamic_dma_scratch_size=1024)
    given = {name: _np.ascontiguousarray(inputs[name]) for name in _INS}
    given["q_cos"], given["q_sin"] = rotary_tables(SQ, 1.0 / _np.sqrt(_np.float32(DH)))
    given["k_cos"], given["k_sin"] = rotary_tables(SK, 1.0)
    arrays, args = {}, []
    for name, a in given.items():
        arrays[f"in_{name}_dram"] = a
        args.append(nc.dram_tensor(f"in_{name}_dram", a.shape, _mybir.dt.from_np(a.dtype), kind="ExternalInput").ap())
    for i, (shape, dtype) in enumerate(_OUTS):
        dt = _mybir.dt.from_np(_np.dtype(dtype))
        args.append(nc.dram_tensor(f"out_{i}_dram", shape, dt, kind="ExternalOutput").ap())
    flamingo_block(nc, *args)
    r = _run(nc, [arrays], core_ids=[0])
    got = tuple(r.results[0][f"out_{i}_dram"] for i in range(len(_OUTS)))
    return got[0]
```
